# Optimizing a Trainium2 kernel written in Bass

```python
import numpy as np
import jax
import jax.numpy as jnp

def _softmax(x, axis=-1):
    return jax.nn.softmax(x, axis=axis)

def _gelu(x):
    return jax.nn.gelu(x, approximate=True)

def _silu(x):
    return jax.nn.silu(x)

def _sigmoid(x):
    return jax.nn.sigmoid(x)

def _layernorm(x, axis=-1, eps=1e-05):
    m = jnp.mean(x, axis=axis, keepdims=True)
    v = jnp.var(x, axis=axis, keepdims=True)
    return (x - m) / jnp.sqrt(v + eps)

def _scatter_add(tgt, idx, src, axis=0):
    return tgt.at[idx].add(src)

def _segment_sum(src, seg, n):
    return jax.ops.segment_sum(src, seg, n)
kernel_name = 'mk_flamingo_gated_d1_seqx_r8_330a80'

def setup_inputs(seed: int=0):
    np.random.seed(seed)
    _w = jnp.asarray

    def _rec_inputs():
        import jax
        import jax.numpy as jnp
        _rk = jax.random.key(seed)
        x = -0.0002928 + 1 * jax.random.normal(jax.random.fold_in(_rk, 1), (8, 128, 128), jnp.float32)
        _lenS = 128 - jax.random.randint(jax.random.fold_in(_rk, 7), (8,), 0, max(1, 128 // 4) + 1, jnp.int32)
        _lenS2 = 128 - jax.random.randint(jax.random.fold_in(_rk, 8), (8,), 0, max(1, 128 // 4) + 1, jnp.int32)
        _ctx_1024P = jax.random.normal(jax.random.fold_in(_rk, 11), (8, 16, 128), jnp.float32)
        _ctx_1024c = jax.random.dirichlet(jax.random.fold_in(_rk, 511), 0.3 * jnp.ones((16,), jnp.float32), (8, 128))
        _ctx_1024t = jnp.einsum('bsk,bkd->bsd', _ctx_1024c, _ctx_1024P)
        _ctx_1024t = _ctx_1024t * jax.lax.rsqrt(jnp.mean(jnp.square(_ctx_1024t)) + 1e-12) * 0.953939
        ctx_1024 = -1.39393e-06 + 0.999914 * (_ctx_1024t + 0.3 * jax.random.normal(jax.random.fold_in(_rk, 611), (8, 128, 128), jnp.float32))
        _g = jax.random.normal(jax.random.fold_in(_rk, 9001), (2, 1), jnp.float32)
        _g = jnp.sign(_g) * jnp.maximum(jnp.abs(_g), 1.0) + (_g == 0) * 1.0
        g_xattn = _g[0]
        g_ffn = _g[1]
        return (x, ctx_1024, g_xattn, g_ffn)
    x, ctx_1024, g_xattn, g_ffn = _rec_inputs()

    def _L0_xattn_setup():
        import jax, jax.numpy as jnp
        import numpy as np
        B, S, D, H = (2, 256, 128, 16)
        HD = D // H
        SCALE = HD ** (-0.5)
        NEG = -1000000000.0
        key = jax.random.key(seed)
        ks = jax.random.split(key, 7)
        w_std = 1.0 / np.sqrt(D)
        return {'query': jax.random.normal(ks[0], (B, S, D), dtype=jnp.float32), 'key': jax.random.normal(ks[1], (B, S, D), dtype=jnp.float32), 'value': jax.random.normal(ks[2], (B, S, D), dtype=jnp.float32), 'Wq': jax.random.normal(ks[3], (D, D), dtype=jnp.float32) * w_std, 'Wk': jax.random.normal(ks[4], (D, D), dtype=jnp.float32) * w_std, 'Wv': jax.random.normal(ks[5], (D, D), dtype=jnp.float32) * w_std, 'Wo': jax.random.normal(ks[6], (D, D), dtype=jnp.float32) * w_std}
    _L0_xattn_all = _L0_xattn_setup()
    _L0_xattn_in = {k: v for k, v in _L0_xattn_all.items() if k in ('Wq', 'Wk', 'Wv', 'Wo')}
    del _L0_xattn_all

    def _L0_ffn_setup():
        import jax, jax.numpy as jnp
        import numpy as np
        LN_EPS = 1e-05

        def _swiglu(h, w_gate_up, w_down):
            gu = h @ w_gate_up.T
            gate, up = jnp.split(gu, 2, axis=-1)
            return jax.nn.silu(gate) * up @ w_down.T
        key = jax.random.key(seed)
        ks = jax.random.split(key, 6)
        d_model, d_ff, E = (128, 512, 8)
        shared_d_ff = d_ff // 4
        routed_d_ff = d_ff - shared_d_ff
        B, S = (4, 256)
        x = jax.random.normal(ks[0], (B, S, d_model), dtype=jnp.float32)
        ln_gamma = jnp.ones((d_model,), jnp.float32)
        ln_beta = jnp.zeros((d_model,), jnp.float32)
        router_w = jax.random.normal(ks[1], (E, d_model), jnp.float32) * 0.02
        gate_up_w = jax.random.normal(ks[2], (E, 2 * routed_d_ff, d_model), jnp.float32) * (1.0 / np.sqrt(d_model))
        down_w = jax.random.normal(ks[3], (E, d_model, routed_d_ff), jnp.float32) * (1.0 / np.sqrt(routed_d_ff))
        shared_gate_up_w = jax.random.normal(ks[4], (2 * shared_d_ff, d_model), jnp.float32) * (1.0 / np.sqrt(d_model))
        shared_down_w = jax.random.normal(ks[5], (d_model, shared_d_ff), jnp.float32) * (1.0 / np.sqrt(shared_d_ff))
        return dict(x=x, ln_gamma=ln_gamma, ln_beta=ln_beta, router_w=router_w, gate_up_w=gate_up_w, down_w=down_w, shared_gate_up_w=shared_gate_up_w, shared_down_w=shared_down_w)
    _L0_ffn_all = _L0_ffn_setup()
    _L0_ffn_in = {k: v for k, v in _L0_ffn_all.items() if k in ('ln_gamma', 'ln_beta', 'router_w', 'gate_up_w', 'down_w', 'shared_gate_up_w', 'shared_down_w')}
    del _L0_ffn_all
    return {'x': x, 'ctx_1024': ctx_1024, 'g_xattn': g_xattn, 'g_ffn': g_ffn, 'L0_xattn_Wq': _L0_xattn_in['Wq'], 'L0_xattn_Wk': _L0_xattn_in['Wk'], 'L0_xattn_Wv': _L0_xattn_in['Wv'], 'L0_xattn_Wo': _L0_xattn_in['Wo'], 'L0_ffn_ln_gamma': _L0_ffn_in['ln_gamma'], 'L0_ffn_ln_beta': _L0_ffn_in['ln_beta'], 'L0_ffn_router_w': _L0_ffn_in['router_w'], 'L0_ffn_gate_up_w': _L0_ffn_in['gate_up_w'], 'L0_ffn_down_w': _L0_ffn_in['down_w'], 'L0_ffn_shared_gate_up_w': _L0_ffn_in['shared_gate_up_w'], 'L0_ffn_shared_down_w': _L0_ffn_in['shared_down_w']}

def reference(x, ctx_1024, g_xattn, g_ffn, L0_xattn_Wq, L0_xattn_Wk, L0_xattn_Wv, L0_xattn_Wo, L0_ffn_ln_gamma, L0_ffn_ln_beta, L0_ffn_router_w, L0_ffn_gate_up_w, L0_ffn_down_w, L0_ffn_shared_gate_up_w, L0_ffn_shared_down_w):
    import jax
    import jax.numpy as jnp

    def _L0_xattn_ref(query, key, value, Wq, Wk, Wv, Wo):
        import jax, jax.numpy as jnp
        import numpy as np
        B, S, D, H = (2, 256, 128, 16)
        HD = D // H
        SCALE = HD ** (-0.5)
        NEG = -1000000000.0
        b, sq, d = query.shape
        sk = key.shape[1]
        q = (query @ Wq.T).reshape(b, sq, H, HD).transpose(0, 2, 1, 3)
        k = (key @ Wk.T).reshape(b, sk, H, HD).transpose(0, 2, 1, 3)
        v = (value @ Wv.T).reshape(b, sk, H, HD).transpose(0, 2, 1, 3)
        scores = jnp.einsum('bhqd,bhkd->bhqk', q, k) * SCALE
        causal = jnp.arange(sq)[:, None] >= jnp.arange(sk)[None, :]
        scores = jnp.where(causal[None, None], scores, NEG)
        attn = jax.nn.softmax(scores, axis=-1)
        out = jnp.einsum('bhqk,bhkd->bhqd', attn, v)
        out = out.transpose(0, 2, 1, 3).reshape(b, sq, d)
        return out @ Wo.T

    def _L0_ffn_ref(x, ln_gamma, ln_beta, router_w, gate_up_w, down_w, shared_gate_up_w, shared_down_w):
        import jax, jax.numpy as jnp
        import numpy as np
        LN_EPS = 1e-05

        def _swiglu(h, w_gate_up, w_down):
            gu = h @ w_gate_up.T
            gate, up = jnp.split(gu, 2, axis=-1)
            return jax.nn.silu(gate) * up @ w_down.T
        B, S, D = x.shape
        E = router_w.shape[0]
        top_k = 2
        xt = x.reshape(-1, D)
        mu = jnp.mean(xt, axis=-1, keepdims=True)
        var = jnp.mean(jnp.square(xt - mu), axis=-1, keepdims=True)
        normed = (xt - mu) * jax.lax.rsqrt(var + LN_EPS) * ln_gamma + ln_beta
        logits = normed.astype(jnp.float32) @ router_w.T
        probs = jax.nn.softmax(logits, axis=-1)
        top_v, top_i = jax.lax.top_k(probs, top_k)
        gates = jax.nn.softmax(top_v, axis=-1)
        comb = jnp.sum(jax.nn.one_hot(top_i, E, dtype=gates.dtype) * gates[..., None], axis=1)
        out = jnp.zeros_like(normed)
        for e in range(E):
            y = _swiglu(normed, gate_up_w[e], down_w[e])
            out = out + comb[:, e, None] * y
        out = out + _swiglu(normed, shared_gate_up_w, shared_down_w)
        return out.reshape(B, S, D)
    x = x + jnp.tanh(g_xattn[0]) * _L0_xattn_ref(_layernorm(x, axis=-1), ctx_1024, ctx_1024, L0_xattn_Wq, L0_xattn_Wk, L0_xattn_Wv, L0_xattn_Wo)
    x = x + jnp.tanh(g_ffn[0]) * _L0_ffn_ref(_layernorm(x, axis=-1), L0_ffn_ln_gamma, L0_ffn_ln_beta, L0_ffn_router_w, L0_ffn_gate_up_w, L0_ffn_down_w, L0_ffn_shared_gate_up_w, L0_ffn_shared_down_w)
    return x

_drawn_inputs = setup_inputs


def setup_inputs(seed=0):
    import zlib

    import numpy as np

    out = dict(_drawn_inputs(seed))
    spreads = {'L0_ffn_ln_gamma': (1.0, 0.2), 'L0_ffn_ln_beta': (0.0, 0.1)}
    factors = {}
    for name, (base, spread) in spreads.items():
        noise = np.random.default_rng([zlib.crc32(name.encode()), seed]).standard_normal(out[name].shape)
        drawn = base * np.exp(spread * noise) if base else spread * noise
        out[name] = jnp.asarray(drawn.astype(out[name].dtype))
    for name, factor in factors.items():
        out[name] = (out[name] * factor).astype(out[name].dtype)
    return out
```

```python
import concourse.bass as bass
from concourse import mybir
from contextlib import ExitStack

B, T, D = 8, 128, 128
H, HD = 16, 8
SETS, ROWS = 4, 4
COPIES = 3
E, F = 8, 384
FC = F // T
SF = 128
PAIRS = 2 * B * T
TILES = PAIRS // T + E - 1
TT = TILES + 1
UNITS = 4 * B
EPS = 1e-5
WX = 2 * F + FC * D
CREDIT = 16
SKIP = 4096.0

WQ, WK, WV, WO, WSG, WSU, WSD, WR = 0, 128, 256, 384, 512, 640, 768, 896
WSMALL = WR + E
C_ID, C_LT, C_CM, C_SL, C_TL = 0, 128, 256, 384, 512
C_LQ, C_LK, C_EW, C_J, C_PK, C_TK, C_ON = 536, 537, 538, 546, 554, 570, 586
CONST = 588


def gated_layer(nc, x_h, ctxT_h, vec_h, wsmall_h, wexp_h, const_h, out_h):
    f32, f32r, bf16, i32 = mybir.dt.float32, mybir.dt.float32r, mybir.dt.bfloat16, mybir.dt.int32
    ALU, ACT, AX = mybir.AluOpType, mybir.ActivationFunctionType, mybir.AxisListType.X
    ctx = ExitStack()
    with ctx:
        def sb(name, shape, dt=f32):
            return ctx.enter_context(nc.sbuf_tensor(name, shape, dt))

        def sem(name):
            return ctx.enter_context(nc.semaphore(name))

        norm_d = nc.dram_tensor("norm_d", (B * T, D), f32, kind="Internal").ap()
        y_d = nc.dram_tensor("y_d", (PAIRS, D), f32, kind="Internal").ap()

        X = sb("X", [T, B * D])
        CT = sb("CT", [D, B * T])
        vec = sb("vec", [T, 2 * D + 2])
        wsm = sb("wsm", [D, WSMALL])
        wsh = sb("wsh", [D, WSMALL], f32r)
        wsl = sb("wsl", [D, WSMALL], f32r)
        wsth = sb("wsth", [D, 2, SETS, 4 * 32], f32r)
        wstl = sb("wstl", [D, 2, SETS, 4 * 32], f32r)
        cst = sb("cst", [T, CONST])
        identb = sb("identb", [T, T], bf16)
        ltb = sb("ltb", [T, T], bf16)
        maskb = sb("maskb", [T, SETS, T], bf16)
        onesb = sb("onesb", [T, T], bf16)
        onesr = sb("onesr", [T, T], f32r)
        slotb = sb("slotb", [T, T], bf16)
        tg = sb("tg", [T, 2])
        st1 = sb("st1", [T, B, 6])
        mv1 = sb("mv1", [T, B, 2])
        ve1 = sb("ve1", [T, B])
        r1 = sb("r1", [T, B])
        mhalf = sb("mhalf", [T, B])
        xn = sb("xn", [T, 2, D])
        xTh = sb("xTh", [D, T], f32r)
        xTl = sb("xTl", [D, T], f32r)
        cTh = sb("cTh", [D, T], f32r)
        cTl = sb("cTl", [D, T], f32r)
        tq = sb("tq", [T, SETS, T], f32r)
        tk = sb("tk", [T, SETS, T], f32r)
        qS = sb("qS", [T, 2, SETS, T], f32r)
        kS = sb("kS", [T, 2, SETS, T], f32r)
        V = sb("V", [T, 2, H, HD + 1])
        nm = sb("nm", [T, 4, SETS])
        R = sb("R", [T, 2, SETS, T], f32r)
        P = sb("P", [T, 4, SETS, T])
        rec = sb("rec", [T, H])
        att = sb("att", [T, D])
        aTh = sb("aTh", [D, T], f32r)
        aTl = sb("aTl", [D, T], f32r)
        X2 = sb("X2", [T, B * D])
        x2 = sb("x2", [T, 2, D])
        st2 = sb("st2", [T, 2, 6])
        mv2 = sb("mv2", [T, 2, 2])
        ve2 = sb("ve2", [T, 2])
        r2 = sb("r2", [T, 2])
        ng = sb("ng", [T, D])
        nr = sb("nr", [T, 2, D])
        NTh = sb("NTh", [D, B * T], f32r)
        NTl = sb("NTl", [D, B * T], f32r)
        wst = sb("wst", [D, 2, WX])
        WH = sb("WH", [D, E * WX], f32r)
        WL = sb("WL", [D, E * WX], f32r)
        lg = sb("lg", [T, B, E])
        col = {n: sb("c_" + n, [T, B]) for n in ("mx", "sum", "rs", "p1", "w1", "p2", "w2", "dp", "e2", "o2", "g1", "g2")}
        ex = sb("ex", [T, B, E])
        pr = sb("pr", [T, B, E])
        eq = sb("eq", [T, 2, B, E])
        ew = sb("ew", [T, 2, B, E])
        M = sb("M", [T, 2, B, E])
        pr2 = sb("pr2", [T, B, E])
        Mb = sb("Mb", [T, B + 1, E], bf16)
        over = sb("over", [T, E, E])
        nt = sb("nt", [T, E])
        inc = sb("inc", [T, E])
        ts = sb("ts", [T, E])
        base = sb("base", [T, E])
        dest = sb("dest", [T, B, E])
        md = sb("md", [T, 2, B, E])
        slot = sb("slot", [T, 2, B])
        sloti = sb("sloti", [T, 2, B], i32)
        inti = sb("inti", [T, 2, 2, B], i32)
        intb = sb("intb", [T, 2 * B], bf16)
        Aoh = sb("Aoh", [T, 2 * B, T], bf16)
        tiles_of = sb("tiles_of", [T, 2 * B, TT])
        Bv = sb("Bv", [T, 2 * B, 2, TT], bf16)
        id1 = sb("id1", [T, TT])
        none = sb("none", [T, TT])
        gi = sb("gi", [T, TT])
        si = sb("si", [T, TT])
        gidx = sb("gidx", [T, TT], i32)
        gtok = sb("gtok", [T, TT], i32)
        sidx = sb("sidx", [T, TT], i32)
        gring = sb("gring", [T, 4], i32)
        sring = sb("sring", [T, 2], i32)
        cmpe = sb("cmpe", [1, TT, E])
        eidf = sb("eidf", [1, TT])
        eid = sb("eid", [1, TT], i32)
        sS = sb("sS", [SF, 2, T])
        sH = sb("sH", [SF, 2, T])
        sHh = sb("sHh", [SF, 2, T], f32r)
        sHl = sb("sHl", [SF, 2, T], f32r)
        XG = sb("XG", [T, 4, D])
        gTh = sb("gTh", [D, 2, T], f32r)
        gTl = sb("gTl", [D, 2, T], f32r)
        gS = sb("gS", [T, 2, F])
        gH = sb("gH", [T, 2, F])
        hTh = sb("hTh", [T, 2, F], f32r)
        hTl = sb("hTl", [T, 2, F], f32r)
        Y = sb("Y", [T, 2, D])
        YG = sb("YG", [T, B, 2, D])
        out_sb = sb("out_sb", [T, B, D])

        bank = [ctx.enter_context(nc.psum_tensor(f"bank{n}", [128, 512], f32)) for n in range(8)]
        Sb, Tb, Ob, Qb, Kb, Mi = bank[0:2], bank[2:4], bank[4], bank[5], bank[6], bank[7]

        ld_x, ld_ctx, ld_small, ld_const, ld_vec = (sem("ld_" + n) for n in ("x", "ctx", "small", "const", "vec"))
        ld_w = [sem(f"ld_w{n}") for n in range(2)]
        st_n = [sem(f"st_n{n}") for n in range(2)]
        pe_S, pe_T, pe_PV, pe_xT, pe_q, pe_k, pe_v, pe_aT, pe_wo, pe_nT = (
            sem("pe_" + n) for n in ("S", "T", "PV", "xT", "q", "k", "v", "aT", "wo", "nT"))
        (v_setup, v_st1, v_ve1, v_xn, v_max, v_xl, v_cl, v_q, v_k, v_rec, v_att, v_al, v_x2, v_st2, v_mv2, v_ve2, v_ng, v_n, v_nl,
         v_wl) = (sem("v_" + n) for n in ("setup", "st1", "ve1", "xn", "max", "xl", "cl", "q", "k", "rec", "att", "al", "x2",
                                          "st2", "mv2", "ve2", "ng", "n", "nl", "wl"))
        a_tg, a_wh, a_xh, a_ch, a_tq, a_tk, a_v, a_exp, a_ah, a_nh, a_eh, a_x2 = (
            sem("a_" + n) for n in ("tg", "wh", "xh", "ch", "tq", "tk", "v", "exp", "ah", "nh", "eh", "x2"))
        p_set, p_r1, p_R, p_mask, p_r2 = (sem("p_" + n) for n in ("set", "r1", "R", "mask", "r2"))
        pe_lg, pe_rank, pe_tab, v_rt, a_ex, a_e2, v_ready = (
            sem(n) for n in ("pe_lg", "pe_rank", "pe_tab", "v_rt", "a_ex", "a_e2", "v_ready"))
        pe_sgu, pe_sy, a_ss, v_sh, a_shh, v_shl, v_x3 = (
            sem(n) for n in ("pe_sgu", "pe_sy", "a_ss", "v_sh", "a_shh", "v_shl", "v_x3"))
        gat = [sem(f"gat{n}") for n in range(4)]
        sca = [sem(f"sca{n}") for n in range(2)]
        pe_gT, pe_gu, pe_hT, pe_y, a_gh, v_gl, a_s, v_h, a_hh, v_hl, a_y = (
            sem(n) for n in ("pe_gT", "pe_gu", "pe_hT", "pe_y", "a_gh", "v_gl", "a_s", "v_h", "a_hh", "v_hl", "a_y"))
        p_go, v_go = sem("p_go"), sem("v_go")
        v_gi, v_si = sem("v_gi"), sem("v_si")
        ld_y = [sem(f"ld_y{n}") for n in range(2)]
        v_f1, v_out, st_o = sem("v_f1"), sem("v_out"), sem("st_o")

        block = ctx.enter_context(nc.Block())

        def at(eng, s, n):
            if not isinstance(n, int) or n > 0:
                eng.wait_ge(s, n)

        def has(b):
            return not isinstance(b, int) or 0 <= b < B

        def seq(b):
            return bass.ds(b * T, T)

        def over_pairs(eng, body):
            body(0)
            with eng.Fori(1, B // 2 - 1) as i:
                body(i)
            body(B // 2 - 1)

        def over_tiles(eng, step):
            mid = (TILES - 3 - 4) // 4 * 4
            for k in range(4):
                step(k, k % 4)
            with eng.Fori(0, mid // 4) as n:
                for m in range(4):
                    step(n * 4 + (m + 4), m)
            for k in range(4 + mid, TILES + 2):
                step(k, k % 4)

        def tile_in(k):
            return not isinstance(k, int) or 0 <= k < TILES

        @block.sync
        def _(sp):
            sp.dma_start(X[:, :].rearrange("p (b d) -> p b d", b=B), x_h.rearrange("(b p) d -> p b d", b=B)).then_inc(ld_x, 16)
            sp.dma_start(wsm[:, :], wsmall_h).then_inc(ld_small, 16)
            sp.dma_start(cst[:, :], const_h).then_inc(ld_const, 16)
            sp.dma_start(CT[:, :], ctxT_h).then_inc(ld_ctx, 16)
            sp.dma_start(vec[:, :], vec_h.to_broadcast((T, 2 * D + 2))).then_inc(ld_vec, 16)

            def load_w(e, c):
                sp.dma_start(wst[:, c, :], wexp_h[bass.ds(e * D, D), :]).then_inc(ld_w[c], 16)

            load_w(0, 0)
            load_w(1, 1)
            for s in st_n:
                sp.sem_inc(s, CREDIT)

            def pair(i):
                for c in range(2):
                    b = 2 * i + c
                    if has(b - 2):
                        sp.wait_ge(v_n, b - 1)
                        sp.dma_start(norm_d[seq(b - 2), :], nr[:, c, :]).then_inc(st_n[c], 16)
                    if has(b + 2):
                        sp.wait_ge(a_eh, b + 1)
                        sp.wait_ge(v_wl, b + 1)
                        load_w(b + 2, c)
            over_pairs(sp, pair)
            for b in (B - 2, B - 1):
                sp.wait_ge(v_n, b + 1)
                sp.dma_start(norm_d[seq(b), :], nr[:, b % 2, :]).then_inc(st_n[b % 2], 16)
            for m in range(2):
                sp.wait_ge(sca[m], 16 * len(range(m, TILES, 2)))
            yv = y_d.rearrange("(b p k) d -> p b (k d)", b=B, k=2)
            for h in range(2):
                bs = slice(h * B // 2, (h + 1) * B // 2)
                sp.dma_start(YG[:, bs, :, :].rearrange("p b k d -> p b (k d)"), yv[:, bs, :]).then_inc(ld_y[h], 16)
            for h in range(2):
                bs = slice(h * B // 2, (h + 1) * B // 2)
                sp.wait_ge(v_out, (h + 1) * B // 2)
                sp.dma_start(out_h.rearrange("(b p) d -> p b d", b=B)[:, bs, :], out_sb[:, bs, :]).then_inc(st_o, 16)
            sp.wait_ge(st_o, 32)

        @block.gpsimd
        def _(pool):
            pool.memset(mhalf[:, :], -0.5).then_inc(p_set, 1)
            pool.memset(V[:, :, :, HD:HD + 1], 1.0).then_inc(p_set, 1)
            pool.memset(Mb[:, B, :], 0.0).then_inc(p_set, 1)
            pool.wait_ge(p_set, 1)
            pool.wait_ge(v_ve1, 1)
            pool.tensor_tensor(r1[:, :], ve1[:, :], mhalf[:, :], ALU.pow).then_inc(p_r1, 1)

            def diag(u, m):
                pool.wait_ge(v_max, u + 1)
                at(pool, pe_T, u - 1)
                pool.sem_inc(p_go, 1)
                pool.affine_select(out=R[:, m % 2], in_=nm[:, m % 4, :].unsqueeze(2).to_broadcast((T, SETS, T)),
                                   pattern=[[0, SETS], [-1, T]], compare_op=ALU.is_equal, fill=0.0, base=0,
                                   channel_multiplier=1).then_inc(p_R, 1)

            def causal(u, m):
                pool.wait_ge(a_exp, u + 1)
                pool.sem_inc(p_go, 1)
                pool.affine_select(out=P[:, m % 4], in_=P[:, m % 4], pattern=[[0, SETS], [1, T]],
                                   compare_op=ALU.is_ge, fill=0.0, base=0, channel_multiplier=-1).then_inc(p_mask, 1)

            def rstd2(b, c):
                pool.wait_ge(v_ve2, b + 1)
                pool.tensor_tensor(r2[:, c:c + 1], ve2[:, c:c + 1], mhalf[:, 0:1], ALU.pow).then_inc(p_r2, 1)

            diag(0, 0)

            def pair(i):
                for c in range(2):
                    b = 2 * i + c
                    for j in range(4):
                        w = 4 * c + j
                        u = 8 * i + w
                        if not (isinstance(u, int) and u + 1 >= UNITS):
                            diag(u + 1, w + 1)
                        if not (isinstance(u, int) and u < 1):
                            causal(u - 1, w - 1)
                        if j == 0 and has(b - 2):
                            rstd2(b - 2, c)
            over_pairs(pool, pair)
            causal(UNITS - 1, UNITS - 1)
            rstd2(B - 2, 0)
            rstd2(B - 1, 1)

            pool.wait_ge(v_ready, 1)
            for c in range(2):
                pool.wait_ge(st_n[c], 16 * B // 2 + CREDIT)

            def gather(k, m):
                pool.wait_ge(v_gi, k + 1)
                at(pool, pe_gT, k - 3)
                pool.sem_inc(p_go, 1)
                pool.indirect_dma_start(XG[:, m, :], None, norm_d, bass.IndirectOffsetOnAxis(gring[:, m:m + 1], 0),
                                        bounds_check=B * T - 1, oob_is_err=False).then_inc(gat[m], 16)

            def scatter(k, m):
                pool.wait_ge(v_si, k + 1)
                pool.wait_ge(a_y, k + 1)
                pool.sem_inc(p_go, 1)
                pool.indirect_dma_start(y_d, bass.IndirectOffsetOnAxis(sring[:, m % 2:m % 2 + 1], 0), Y[:, m % 2, :], None,
                                        bounds_check=PAIRS - 1, oob_is_err=False).then_inc(sca[m % 2], 16)
            for k in range(3):
                gather(k, k)

            def step(k, m):
                if tile_in(k + 3):
                    gather(k + 3, (m + 3) % 4)
                if tile_in(k - 2):
                    scatter(k - 2, (m - 2) % 4)
            over_tiles(pool, step)

        @block.scalar
        def _(act):
            act.wait_ge(ld_small, 16)
            act.activation(wsh[:, :], wsm[:, :], ACT.Copy).then_inc(a_wh, 1)
            act.wait_ge(ld_vec, 16)
            act.activation(tg[:, :], vec[:, 2 * D:2 * D + 2], ACT.Tanh).then_inc(a_tg, 1)

            def ctx_hi(b):
                at(act, pe_v, b)
                act.activation(cTh[:, :], CT[:, seq(b)], ACT.Copy).then_inc(a_ch, 1)

            def x_hi(b):
                act.wait_ge(pe_xT, b + 1)
                at(act, pe_q, b)
                act.activation(xTh[:, :], Mi[:, 0:T], ACT.Copy).then_inc(a_xh, 1)

            def qkv(b, c):
                act.wait_ge(pe_q, b + 1)
                at(act, v_q, b)
                act.activation(tq[:, :, :], Qb[:, :].rearrange("p (s t) -> p s t", s=SETS), ACT.Copy,
                               scale=cst[:, C_LQ:C_LQ + 1]).then_inc(a_tq, 1)
                act.wait_ge(pe_k, b + 1)
                at(act, v_k, b)
                act.activation(tk[:, :, :], Kb[:, :].rearrange("p (s t) -> p s t", s=SETS), ACT.Copy,
                               scale=cst[:, C_LK:C_LK + 1]).then_inc(a_tk, 1)
                act.wait_ge(pe_v, b + 1)
                at(act, pe_PV, 4 * (b - 1))
                act.activation(V[:, c, :, 0:HD], Mi[:, 0:D].rearrange("p (h e) -> p h e", h=H), ACT.Copy).then_inc(a_v, 1)

            def expo(u, m):
                act.wait_ge(pe_T, u + 1)
                at(act, pe_PV, u - 3)
                act.activation(P[:, m % 4], Tb[m % 2][:, :].rearrange("p (s t) -> p s t", s=SETS), ACT.Exp).then_inc(a_exp, 1)

            def att_hi(b):
                act.wait_ge(pe_aT, b + 1)
                at(act, pe_wo, b)
                act.activation(aTh[:, :], Mi[:, 0:T], ACT.Copy).then_inc(a_ah, 1)

            def keep(b, c):
                act.wait_ge(v_x2, b + 1)
                act.activation(X2[:, seq(b)], x2[:, c, :], ACT.Copy).then_inc(a_x2, 1)

            def n_hi(b):
                act.wait_ge(pe_nT, b + 1)
                act.activation(NTh[:, seq(b)], Qb[:, 0:T], ACT.Copy).then_inc(a_nh, 1)

            def w_hi(e, c, ep):
                act.wait_ge(ld_w[c], ep)
                act.activation(WH[:, bass.ds(e * WX, WX)], wst[:, c, :], ACT.Copy).then_inc(a_eh, 1)

            act.wait_ge(ld_ctx, 16)
            act.wait_ge(ld_const, 16)
            ctx_hi(0)
            x_hi(0)
            qkv(0, 0)

            def pair(i):
                for c in range(2):
                    b = 2 * i + c
                    for j in range(4):
                        w = 4 * c + j
                        u = 8 * i + w
                        if j == 0 and has(b + 1):
                            ctx_hi(b + 1)
                            x_hi(b + 1)
                        if j == 1 and has(b + 1):
                            qkv(b + 1, 1 - c)
                        if j == 3 and has(b - 1):
                            att_hi(b - 1)
                        if j == 3 and has(b - 2):
                            n_hi(b - 2)
                        if j == 2 and has(b - 2):
                            keep(b - 2, c)
                        expo(u, w)
                        if j == 2:
                            w_hi(b, c, 16 * i + 16)
            over_pairs(act, pair)
            att_hi(B - 1)
            keep(B - 2, 0)
            n_hi(B - 2)
            keep(B - 1, 1)
            n_hi(B - 1)

            act.wait_ge(v_rt, 2)
            act.activation(ex[:, :, :], lg[:, :, :], ACT.Exp).then_inc(a_ex, 1)
            act.wait_ge(v_rt, V_DP)
            act.activation(col["e2"][:, :], col["dp"][:, :], ACT.Exp).then_inc(a_e2, 1)

            def shared(b, c):
                act.wait_ge(pe_sgu, b + 1)
                at(act, v_sh, b - 1)
                act.activation(sS[:, c, :], bank[c][:, 0:T], ACT.Silu).then_inc(a_ss, 1)
                act.wait_ge(v_sh, b + 1)
                at(act, pe_sy, b - 1)
                act.activation(sHh[:, c, :], sH[:, c, :], ACT.Copy).then_inc(a_shh, 1)

            for b in range(2):
                shared(b, b)
            with act.Fori(1, B // 2) as i:
                for c in range(2):
                    shared(2 * i + c, c)

            def tok_hi(k, m):
                act.wait_ge(pe_gT, k + 1)
                at(act, pe_gu, k - 1)
                act.activation(gTh[:, m % 2, :], bank[4][:, 0:T], ACT.Copy).then_inc(a_gh, 1)

            tok_hi(0, 0)

            def step(k, m):
                if tile_in(k - 1):
                    act.wait_ge(pe_hT, k)
                    at(act, pe_y, k - 2)
                    act.activation(hTh[:, (m - 1) % 2, :], bank[5 + (m - 1) % 2][:, 0:F], ACT.Copy).then_inc(a_hh, 1)
                if tile_in(k + 1):
                    tok_hi(k + 1, m + 1)
                if tile_in(k - 2):
                    act.wait_ge(pe_y, k - 1)
                    at(act, sca[m % 2], 16 * ((k - 2) // 2))
                    act.activation(Y[:, m % 2, :], bank[7][:, 0:D], ACT.Copy).then_inc(a_y, 1)
                if tile_in(k):
                    act.wait_ge(pe_gu, k + 1)
                    at(act, v_h, k - 1)
                    act.activation(gS[:, m % 2, :], bank[m % 2][:, 0:F], ACT.Silu).then_inc(a_s, 1)
            over_tiles(act, step)

        @block.vector
        def _(dve):
            dve.wait_ge(ld_x, 16)
            for b in range(B):
                dve.bn_stats(st1[:, b, :], X[:, b * D:(b + 1) * D]).then_inc(v_st1, 1)
            for b in range(B):
                dve.wait_ge(v_st1, b + 1)
                dve.bn_aggr(mv1[:, b, :], st1[:, b, :]).then_inc(v_st1, 1)
            dve.wait_ge(v_st1, 2 * B)
            dve.tensor_scalar(ve1[:, :], mv1[:, :, 1], EPS, None, ALU.add).then_inc(v_ve1, 1)
            dve.wait_ge(ld_const, 16)
            for dst, src in ((identb[:, :], C_ID), (ltb[:, :], C_LT), (slotb[:, :], C_SL)):
                dve.tensor_copy(dst, cst[:, src:src + T]).then_inc(v_setup, 1)
            dve.tensor_copy(maskb[:, :, :], cst[:, C_CM:C_CM + T].unsqueeze(1).to_broadcast((T, SETS, T))).then_inc(v_setup, 1)
            dve.tensor_copy(onesr[:, :], cst[:, C_ON:C_ON + 1].to_broadcast((T, T))).then_inc(v_setup, 1)
            dve.tensor_copy(onesb[:, :], cst[:, C_ON:C_ON + 1].to_broadcast((T, T))).then_inc(v_setup, 1)
            dve.wait_ge(a_wh, 1)
            dve.tensor_tensor(wsl[:, :], wsm[:, :], wsh[:, :].bitcast(f32), ALU.subtract).then_inc(v_setup, 1)
            dve.wait_ge(v_setup, 7)
            for dst, src in ((wsth, wsh), (wstl, wsl)):
                for n in range(2):
                    dve.memset(dst[:, n].bitcast(f32), 0.0).then_inc(v_setup, 1)
            dve.wait_ge(v_setup, 11)
            for dst, src in ((wsth, wsh), (wstl, wsl)):
                for n, o in ((0, WQ), (1, WK)):
                    for r in range(COPIES):
                        d = dst[:, n].rearrange("p s (j r e) -> p (s j) r e", j=ROWS, e=HD)
                        s = src[:, o:o + D].rearrange("p (h e) -> p h e", e=HD).bitcast(f32)
                        dve.tensor_copy(d[:, :, r, :], s).then_inc(v_setup, 1)

            def normalise(b, c):
                at(dve, pe_xT, b - 1)
                dve.tensor_scalar(xn[:, c, :], X[:, seq(b)], mv1[:, bass.ds(b, 1), 0], r1[:, bass.ds(b, 1)],
                                  ALU.subtract, ALU.mult).then_inc(v_xn, 1)

            def x_ctx_lo(b):
                dve.wait_ge(a_ch, b + 1)
                at(dve, pe_v, b)
                dve.tensor_tensor(cTl[:, :], CT[:, seq(b)], cTh[:, :].bitcast(f32), ALU.subtract).then_inc(v_cl, 1)
                dve.wait_ge(a_xh, b + 1)
                at(dve, pe_q, b)
                dve.tensor_tensor(xTl[:, :], Mi[:, 0:T], xTh[:, :].bitcast(f32), ALU.subtract).then_inc(v_xl, 1)

            def stack(b, c):
                dve.wait_ge(a_tq, b + 1)
                at(dve, pe_T, 4 * (b - 1))
                dve.scalar_tensor_tensor(qS[:, c], Qb[:, :].rearrange("p (s t) -> p s t", s=SETS), HD ** -0.5,
                                         tq[:, :, :].bitcast(f32), ALU.mult, ALU.subtract).then_inc(v_q, 1)
                dve.wait_ge(a_tk, b + 1)
                dve.tensor_tensor(kS[:, c], Kb[:, :].rearrange("p (s t) -> p s t", s=SETS), tk[:, :, :].bitcast(f32),
                                  ALU.subtract).then_inc(v_k, 1)

            def negmax(u, m):
                dve.wait_ge(pe_S, u + 1)
                at(dve, p_R, u - 3)
                dve.tensor_reduce(nm[:, m % 4, :], Sb[m % 2][:, :].rearrange("p (s t) -> p s t", s=SETS), AX, ALU.max,
                                  negate=True).then_inc(v_max, 1)

            def weigh(b):
                o = Ob[:, 0:H * (HD + 1)].rearrange("p (h e) -> p h e", h=H)
                dve.wait_ge(pe_PV, 4 * b + 4)
                dve.reciprocal(rec[:, :], o[:, :, HD]).then_inc(v_rec, 1)
                dve.wait_ge(v_rec, b + 1)
                at(dve, pe_aT, b)
                dve.tensor_tensor(att[:, :].rearrange("p (h e) -> p h e", h=H), o[:, :, 0:HD],
                                  rec[:, :].unsqueeze(2).to_broadcast((T, H, HD)), ALU.mult).then_inc(v_att, 1)

            def att_lo(b):
                dve.wait_ge(a_ah, b + 1)
                at(dve, pe_wo, b)
                dve.tensor_tensor(aTl[:, :], Mi[:, 0:T], aTh[:, :].bitcast(f32), ALU.subtract).then_inc(v_al, 1)

            def residual(b, c):
                dve.wait_ge(pe_wo, b + 1)
                dve.scalar_tensor_tensor(x2[:, c, :], Mi[:, 0:D], tg[:, 0:1], X[:, seq(b)], ALU.mult, ALU.add).then_inc(v_x2, 1)
                dve.wait_ge(v_x2, b + 1)
                dve.bn_stats(st2[:, c, :], x2[:, c, :]).then_inc(v_st2, 1)
                dve.wait_ge(v_st2, b + 1)
                dve.sem_inc(v_go, 1)
                dve.bn_aggr(mv2[:, c, :], st2[:, c, :]).then_inc(v_mv2, 1)
                dve.wait_ge(v_mv2, b + 1)
                dve.tensor_scalar(ve2[:, c:c + 1], mv2[:, c, 1:2], 1.0 + EPS, EPS * EPS, ALU.mult, ALU.add).then_inc(v_ve2, 1)

            def normed(b, c):
                dve.scalar_tensor_tensor(ng[:, :], x2[:, c, :], mv2[:, c, 0:1], vec[:, 0:D], ALU.subtract,
                                         ALU.mult).then_inc(v_ng, 1)
                dve.wait_ge(v_ng, b + 1)
                dve.wait_ge(p_r2, b + 1)
                dve.wait_ge(st_n[c], 8 * (b - c) + CREDIT)
                dve.scalar_tensor_tensor(nr[:, c, :], ng[:, :], r2[:, c:c + 1], vec[:, D:2 * D], ALU.mult,
                                         ALU.add).then_inc(v_n, 1)

            def n_lo(b):
                dve.wait_ge(a_nh, b + 1)
                dve.tensor_tensor(NTl[:, seq(b)], Qb[:, 0:T], NTh[:, seq(b)].bitcast(f32), ALU.subtract).then_inc(v_nl, 1)

            def w_lo(e, c):
                dve.wait_ge(a_eh, e + 1)
                dve.tensor_tensor(WL[:, bass.ds(e * WX, WX)], wst[:, c, :], WH[:, bass.ds(e * WX, WX)].bitcast(f32),
                                  ALU.subtract).then_inc(v_wl, 1)

            dve.wait_ge(p_r1, 1)
            normalise(0, 0)
            normalise(1, 1)
            dve.wait_ge(ld_ctx, 16)
            x_ctx_lo(0)
            stack(0, 0)
            dve.wait_ge(a_tg, 1)
            negmax(0, 0)

            def pair(i):
                for c in range(2):
                    b = 2 * i + c
                    for j in range(4):
                        w = 4 * c + j
                        u = 8 * i + w
                        if not (isinstance(u, int) and u + 1 >= UNITS):
                            negmax(u + 1, w + 1)
                        if j == 0:
                            if has(b - 2):
                                residual(b - 2, c)
                            if has(b + 1):
                                x_ctx_lo(b + 1)
                        if j == 1:
                            if has(b + 1):
                                stack(b + 1, 1 - c)
                            if has(b - 2):
                                normed(b - 2, c)
                        if j == 2:
                            if has(b - 1):
                                weigh(b - 1)
                            if has(b + 2):
                                normalise(b + 2, c)
                        if j == 3:
                            if has(b - 1):
                                att_lo(b - 1)
                            if has(b - 2):
                                n_lo(b - 2)
                            w_lo(b, c)
            over_pairs(dve, pair)
            residual(B - 2, 0)
            weigh(B - 1)
            normed(B - 2, 0)
            att_lo(B - 1)
            n_lo(B - 2)
            residual(B - 1, 1)
            normed(B - 1, 1)
            n_lo(B - 1)

            done = [0]

            def link(ins):
                done[0] += 1
                ins.then_inc(v_rt, 1)
                dve.wait_ge(v_rt, done[0])

            def wide(a):
                return a.unsqueeze(2).to_broadcast((T, B, E))

            lgp = bank[0][:, 0:B * E].rearrange("p (b e) -> p b e", b=B)
            dve.wait_ge(pe_lg, 1)
            link(dve.tensor_reduce(col["mx"][:, :], lgp, AX, ALU.max))
            link(dve.tensor_tensor(lg[:, :, :], lgp, wide(col["mx"][:, :]), ALU.subtract))
            dve.wait_ge(a_ex, 1)
            link(dve.tensor_reduce(col["sum"][:, :], ex[:, :, :], AX, ALU.add))
            link(dve.reciprocal(col["rs"][:, :], col["sum"][:, :]))
            link(dve.tensor_tensor(pr[:, :, :], ex[:, :, :], wide(col["rs"][:, :]), ALU.mult))
            for n, src in ((0, pr), (1, pr2)):
                p, wn = col[f"p{n + 1}"], col[f"w{n + 1}"]
                if n:
                    link(dve.scalar_tensor_tensor(pr2[:, :, :], M[:, 0], -2.0, pr[:, :, :], ALU.mult, ALU.add))
                link(dve.tensor_reduce(p[:, :], src[:, :, :], AX, ALU.max))
                link(dve.tensor_tensor(eq[:, n], src[:, :, :], wide(p[:, :]), ALU.is_equal))
                link(dve.tensor_tensor(ew[:, n], eq[:, n], cst[:, C_EW:C_EW + E].unsqueeze(1).to_broadcast((T, B, E)), ALU.mult))
                link(dve.tensor_reduce(wn[:, :], ew[:, n], AX, ALU.max))
                link(dve.tensor_tensor(M[:, n], ew[:, n], wide(wn[:, :]), ALU.is_equal))
            dve.wait_ge(p_set, 3)
            link(dve.tensor_tensor(Mb[:, 0:B, :], M[:, 0], M[:, 1], ALU.add))
            assert done[0] == V_MB
            link(dve.tensor_tensor(col["dp"][:, :], col["p2"][:, :], col["p1"][:, :], ALU.subtract))
            assert done[0] == V_DP
            dve.wait_ge(pe_rank, 1)
            rank = bank[1][:, 0:(B + 1) * E].rearrange("p (b e) -> p b e", e=E)
            link(dve.tensor_tensor(over[:, :, :], rank[:, B, :].unsqueeze(2).to_broadcast((T, E, E)),
                                   cst[:, C_J:C_J + E].unsqueeze(1).to_broadcast((T, E, E)), ALU.is_gt))
            link(dve.tensor_reduce(nt[:, :], over[:, :, :], AX, ALU.add))
            link(dve.tensor_tensor_scan(inc[:, :], cst[:, C_ON:C_ON + 1].to_broadcast((T, E)), nt[:, :], 0.0, ALU.mult, ALU.add))
            link(dve.tensor_tensor(ts[:, :], inc[:, :], nt[:, :], ALU.subtract))
            link(dve.tensor_scalar(base[:, :], ts[:, :], float(T), None, ALU.mult))
            link(dve.tensor_tensor(dest[:, :, :], rank[:, 0:B, :], base[:, :].unsqueeze(1).to_broadcast((T, B, E)), ALU.add))
            for n in range(2):
                link(dve.tensor_tensor(md[:, n], M[:, n], dest[:, :, :], ALU.mult))
            link(dve.tensor_reduce(slot[:, :, :], md[:, :, :, :], AX, ALU.add))
            link(dve.tensor_copy(sloti[:, :, :], slot[:, :, :]))
            link(dve.tensor_scalar(inti[:, 0], sloti[:, :, :], T - 1, None, ALU.bitwise_and))
            link(dve.tensor_scalar(inti[:, 1], sloti[:, :, :], T.bit_length() - 1, None, ALU.arith_shift_right))
            link(dve.tensor_copy(intb[:, :], inti[:, 0].rearrange("p k b -> p (k b)")))
            link(dve.tensor_tensor(Aoh[:, :, :], slotb[:, :].unsqueeze(1).to_broadcast((T, 2 * B, T)),
                                   intb[:, :].unsqueeze(2).to_broadcast((T, 2 * B, T)), ALU.is_equal))
            link(dve.tensor_tensor(tiles_of[:, :, :], cst[:, C_TL:C_TL + TT].unsqueeze(1).to_broadcast((T, 2 * B, TT)),
                                   inti[:, 1].rearrange("p k b -> p (k b)").unsqueeze(2).to_broadcast((T, 2 * B, TT)), ALU.is_equal))
            for n, o in ((0, C_PK), (1, C_TK)):
                link(dve.tensor_tensor(Bv[:, :, n, :], tiles_of[:, :, :],
                                       cst[:, o:o + 2 * B].unsqueeze(2).to_broadcast((T, 2 * B, TT)), ALU.mult))
            assert done[0] == V_BV
            link(dve.tensor_tensor(cmpe[:, :, 0:E - 1], cst[0:1, C_TL:C_TL + TT].unsqueeze(2).to_broadcast((1, TT, E - 1)),
                                   ts[0:1, 1:E].unsqueeze(1).to_broadcast((1, TT, E - 1)), ALU.is_ge))
            link(dve.tensor_reduce(eidf[:, :], cmpe[:, :, 0:E - 1], AX, ALU.add))
            link(dve.tensor_copy(eid[:, :], eidf[:, :]))
            dve.wait_ge(a_e2, 1)
            link(dve.tensor_scalar(col["o2"][:, :], col["e2"][:, :], 1.0, None, ALU.add))
            link(dve.reciprocal(col["g1"][:, :], col["o2"][:, :]))
            link(dve.tensor_tensor(col["g2"][:, :], col["e2"][:, :], col["g1"][:, :], ALU.mult))
            dve.wait_ge(pe_tab, 1)
            tab = bank[2][:, 0:2 * TT].rearrange("p (n i) -> p n i", n=2)
            link(dve.tensor_reduce(id1[:, :], tab.rearrange("p n i -> p i n"), AX, ALU.add))
            link(dve.tensor_scalar(gi[:, :], id1[:, :], -1.0, 0.0, ALU.add, ALU.max))
            link(dve.tensor_copy(gidx[:, :], gi[:, :]))
            link(dve.tensor_scalar(gtok[:, :], gidx[:, :], 1, None, ALU.arith_shift_right))
            link(dve.tensor_scalar(none[:, :], id1[:, :], 0.0, SKIP, ALU.is_equal, ALU.mult))
            link(dve.tensor_tensor(si[:, :], gi[:, :], none[:, :], ALU.add))
            dve.tensor_copy(sidx[:, :], si[:, :]).then_inc(v_ready, 1)

            def shared(b, c):
                dve.wait_ge(a_ss, b + 1)
                at(dve, v_shl, b - 1)
                at(dve, a_shh, b - 1)
                dve.tensor_tensor(sH[:, c, :], sS[:, c, :], bank[2 + c][:, 0:T], ALU.mult).then_inc(v_sh, 1)
                dve.wait_ge(a_shh, b + 1)
                at(dve, pe_sy, b - 1)
                dve.tensor_tensor(sHl[:, c, :], sH[:, c, :], sHh[:, c, :].bitcast(f32), ALU.subtract).then_inc(v_shl, 1)
                dve.wait_ge(pe_sy, b + 1)
                dve.scalar_tensor_tensor(X2[:, seq(b)], bank[4 + c][:, 0:D], tg[:, 1:2], X2[:, seq(b)], ALU.mult,
                                         ALU.add).then_inc(v_x3, 1)
            for b in range(2):
                shared(b, b)
            with dve.Fori(1, B // 2) as i:
                for c in range(2):
                    shared(2 * i + c, c)

            def tok_lo(k, m):
                dve.wait_ge(a_gh, k + 1)
                at(dve, pe_gu, k - 1)
                dve.tensor_tensor(gTl[:, m % 2, :], bank[4][:, 0:T], gTh[:, m % 2, :].bitcast(f32), ALU.subtract).then_inc(v_gl, 1)

            def indices(k, m, ep):
                if not isinstance(k, int) or k >= 4:
                    dve.wait_ge(gat[m], ep)
                dve.tensor_copy(gring[:, m:m + 1], gtok[:, bass.ds(k, 1)]).then_inc(v_gi, 1)

            def out_indices(k, m):
                at(dve, sca[m % 2], k // 2 * 16)
                dve.tensor_copy(sring[:, m % 2:m % 2 + 1], sidx[:, bass.ds(k, 1)]).then_inc(v_si, 1)

            for k in range(3):
                indices(k, k, 0)
            tok_lo(0, 0)

            def step(k, m):
                if tile_in(k + 3):
                    indices(k + 3, (m + 3) % 4, (k + 3) // 4 * 16)
                if tile_in(k - 2):
                    out_indices(k - 2, (m - 2) % 4)
                if tile_in(k - 1):
                    dve.wait_ge(a_hh, k)
                    at(dve, pe_y, k - 2)
                    dve.tensor_tensor(hTl[:, (m - 1) % 2, :], bank[5 + (m - 1) % 2][:, 0:F], hTh[:, (m - 1) % 2, :].bitcast(f32),
                                      ALU.subtract).then_inc(v_hl, 1)
                if tile_in(k + 1):
                    tok_lo(k + 1, m + 1)
                if tile_in(k):
                    dve.wait_ge(a_s, k + 1)
                    at(dve, pe_hT, k - 1)
                    dve.tensor_tensor(gH[:, m % 2, :], gS[:, m % 2, :], bank[2 + m % 2][:, 0:F], ALU.mult).then_inc(v_h, 1)
            over_tiles(dve, step)

            dve.wait_ge(v_rt, done[0])
            for h in range(2):
                dve.wait_ge(ld_y[h], 16)
                bs = range(h * B // 2, (h + 1) * B // 2)
                for k in range(2):
                    for b in bs:
                        dve.tensor_scalar(YG[:, b, k, :], YG[:, b, k, :], col[f"g{k + 1}"][:, b:b + 1], tg[:, 1:2], ALU.mult,
                                          ALU.mult).then_inc(v_f1, 1)
                dve.wait_ge(v_f1, h * (B + 1) + B)
                dve.tensor_tensor(YG[:, bs[0]:bs[-1] + 1, 0, :], YG[:, bs[0]:bs[-1] + 1, 0, :],
                                  YG[:, bs[0]:bs[-1] + 1, 1, :], ALU.add).then_inc(v_f1, 1)
                dve.wait_ge(v_f1, (h + 1) * (B + 1))
                for b in bs:
                    dve.tensor_tensor(out_sb[:, b, :], YG[:, b, 0, :], X2[:, b * D:(b + 1) * D], ALU.add).then_inc(v_out, 1)

        @block.tensor
        def _(pe):
            def split3(out, ah, al, bh, bl, start=True, stop=True):
                pe.matmul(out, ah, bh, start=start, stop=False)
                pe.matmul(out, ah, bl, start=False, stop=False)
                return pe.matmul(out, al, bh, start=False, stop=stop)

            ident = cst[:, C_ID:C_ID + T]

            def x_T(b, c):
                pe.wait_ge(v_xn, b + 1)
                at(pe, a_v, b)
                pe.transpose(Mi[:, 0:T], xn[:, c, :], ident).then_inc(pe_xT, 1)

            def qkv(b):
                pe.wait_ge(a_xh, b + 1)
                pe.wait_ge(v_xl, b + 1)
                for s in range(SETS):
                    last = split3(Qb[:, s * T:(s + 1) * T], wsth[:, 0, s, :], wstl[:, 0, s, :], xTh[:, :], xTl[:, :])
                last.then_inc(pe_q, 1)
                pe.wait_ge(a_ch, b + 1)
                pe.wait_ge(v_cl, b + 1)
                at(pe, v_k, b)
                for s in range(SETS):
                    last = split3(Kb[:, s * T:(s + 1) * T], wsth[:, 1, s, :], wstl[:, 1, s, :], cTh[:, :], cTl[:, :])
                last.then_inc(pe_k, 1)
                split3(Mi[:, 0:D], cTh[:, :], cTl[:, :], wsh[:, WV:WV + D], wsl[:, WV:WV + D]).then_inc(pe_v, 1)

            def scores(u, b, c, j, m):
                pe.wait_ge(v_q, b + 1)
                pe.wait_ge(v_k, b + 1)
                at(pe, v_max, u - 1)
                r = slice(32 * j, 32 * j + COPIES * HD)
                pe.matmul(Sb[m % 2][:, :], identb[:, :], maskb[:, :, :].rearrange("p s t -> p (s t)"), start=True, stop=False)
                for s in range(SETS):
                    last = pe.matmul(Sb[m % 2][:, s * T:(s + 1) * T], qS[r, c, s, :], kS[r, c, s, :], start=False,
                                     stop=(s == SETS - 1))
                last.then_inc(pe_S, 1)

            def scores_T(u, c, j, m):
                at(pe, a_exp, u - 1)
                r = slice(32 * j, 32 * j + COPIES * HD)
                for s in range(SETS):
                    pe.matmul(Tb[m % 2][:, s * T:(s + 1) * T], kS[r, c, s, :], qS[r, c, s, :], start=(s == 0), stop=False)
                pe.wait_ge(p_R, u + 1)
                pe.matmul(Tb[m % 2][:, :], onesr[:, :], R[:, m % 2].rearrange("p s t -> p (s t)"), start=False,
                          stop=True).then_inc(pe_T, 1)

            def values(u, b, c, j, m):
                pe.wait_ge(p_mask, u + 1)
                if j == 0:
                    pe.wait_ge(a_v, b + 1)
                    at(pe, v_att, b)
                for s in range(SETS):
                    h = SETS * s + j
                    last = pe.matmul(Ob[:, h * (HD + 1):(h + 1) * (HD + 1)], P[:, m % 4, s, :], V[:, c, h, :],
                                     start=(j == 0 and s == 0), stop=(j == ROWS - 1 and s == SETS - 1))
                last.then_inc(pe_PV, 1)

            def att_T(b, vb):
                pe.wait_ge(v_att, b + 1)
                pe.wait_ge(a_v, vb)
                pe.transpose(Mi[:, 0:T], att[:, :], ident).then_inc(pe_aT, 1)

            def out_proj(b):
                pe.wait_ge(a_ah, b + 1)
                pe.wait_ge(v_al, b + 1)
                split3(Mi[:, 0:D], aTh[:, :], aTl[:, :], wsh[:, WO:WO + D], wsl[:, WO:WO + D]).then_inc(pe_wo, 1)

            def n_T(b, c, qb):
                pe.wait_ge(v_n, b + 1)
                pe.wait_ge(v_q, qb)
                if isinstance(b, int):
                    at(pe, v_nl, b)
                pe.transpose(Qb[:, 0:T], nr[:, c, :], ident).then_inc(pe_nT, 1)

            pe.wait_ge(v_setup, 11 + 4 * COPIES)
            x_T(0, 0)
            qkv(0)
            pe.wait_ge(p_set, 2)
            scores(0, 0, 0, 0, 0)

            def pair(i):
                for c in range(2):
                    b = 2 * i + c
                    for j in range(4):
                        w = 4 * c + j
                        u = 8 * i + w
                        if j < 3:
                            scores(u + 1, b, c, j + 1, w + 1)
                        elif has(b + 1):
                            scores(u + 1, b + 1, 1 - c, 0, w + 1)
                        if not (isinstance(u, int) and u < 2):
                            if j < 2:
                                values(u - 2, b - 1, 1 - c, j + 2, w - 2)
                            else:
                                values(u - 2, b, c, j - 2, w - 2)
                        if j == 0 and has(b + 1):
                            at(pe, v_x2, b - 1)
                            x_T(b + 1, 1 - c)
                        if j == 1 and has(b + 1):
                            qkv(b + 1)
                        if j == 3 and has(b - 2):
                            n_T(b - 2, c, b + 2 if has(b + 1) else B)
                        scores_T(u, c, j, w)
                        if j == 2 and has(b - 1):
                            att_T(b - 1, b + 2 if has(b + 1) else B)
                        if j == 3 and has(b - 1):
                            out_proj(b - 1)
            over_pairs(pe, pair)
            for j in (2, 3):
                values(UNITS - 4 + j, B - 1, 1, j, UNITS - 4 + j)
            pe.wait_ge(v_x2, B - 1)
            att_T(B - 1, B)
            n_T(B - 2, 0, B)
            out_proj(B - 1)
            n_T(B - 1, 1, B)

            for b in range(B):
                pe.wait_ge(a_nh, b + 1)
                pe.wait_ge(v_nl, b + 1)
                last = split3(bank[0][:, b * E:(b + 1) * E], NTh[:, b * T:(b + 1) * T], NTl[:, b * T:(b + 1) * T],
                              wsh[:, WR:WR + E], wsl[:, WR:WR + E])
            last.then_inc(pe_lg, 1)

            pe.wait_ge(v_rt, V_MB)
            mb = Mb[:, :, :].rearrange("p b e -> p (b e)")
            pe.matmul(bank[1][:, 0:(B + 1) * E], ltb[:, :], mb, start=True, stop=False)
            for s in range(1, B + 1):
                last = pe.matmul(bank[1][:, s * E:(B + 1) * E], onesb[:, :], mb[:, 0:(B + 1 - s) * E], start=False, stop=(s == B))
            last.then_inc(pe_rank, 1)
            pe.wait_ge(v_rt, V_BV)
            for n in range(2 * B):
                last = pe.matmul(bank[2][:, 0:2 * TT], Aoh[:, n, :], Bv[:, n].rearrange("p n i -> p (n i)"), start=(n == 0),
                                 stop=(n == 2 * B - 1))
            last.then_inc(pe_tab, 1)

            def shared_in(b, c):
                at(pe, a_ss, b - 1)
                at(pe, v_sh, b - 1)
                for o, bk in ((WSG, bank[c]), (WSU, bank[2 + c])):
                    last = split3(bk[:, 0:T], wsh[:, o:o + SF], wsl[:, o:o + SF], NTh[:, seq(b)], NTl[:, seq(b)])
                last.then_inc(pe_sgu, 1)

            def shared_out(b, c):
                pe.wait_ge(a_shh, b + 1)
                pe.wait_ge(v_shl, b + 1)
                at(pe, v_x3, b - 1)
                split3(bank[4 + c][:, 0:D], sHh[:, c, :], sHl[:, c, :], wsh[:, WSD:WSD + D], wsl[:, WSD:WSD + D]).then_inc(pe_sy, 1)
            pe.wait_ge(v_ready, 1)

            def shared_pair(i):
                for c in range(2):
                    shared_in(2 * i + c, c)
                for c in range(2):
                    shared_out(2 * i + c, c)
            shared_pair(0)
            with pe.Fori(1, B // 2) as i:
                shared_pair(i)

            def tok_T(k, m, ep):
                pe.wait_ge(gat[m], ep)
                at(pe, v_gl, k)
                pe.transpose(bank[4][:, 0:T], XG[:, m, :], ident).then_inc(pe_gT, 1)

            pe.wait_ge(v_x3, B)
            pe.wait_ge(a_eh, E)
            pe.wait_ge(v_wl, E)
            tok_T(0, 0, 16)

            def step(k, m):
                if tile_in(k):
                    e = pe.value_load(eid[0:1, bass.ds(k, 1)], min_val=0, max_val=E - 1)
                    pe.wait_ge(a_gh, k + 1)
                    pe.wait_ge(v_gl, k + 1)
                    at(pe, a_s, k - 1)
                    at(pe, v_h, k - 1)
                    gh, gl = gTh[:, m % 2, :], gTl[:, m % 2, :]
                    for n, bk in ((0, bank[m % 2]), (1, bank[2 + m % 2])):
                        w = bass.ds(e * WX + n * F, F)
                        last = split3(bk[:, 0:F], gh, gl, WH[:, w], WL[:, w])
                    last.then_inc(pe_gu, 1)
                if tile_in(k - 1):
                    pe.wait_ge(v_h, k)
                    at(pe, v_hl, k - 2)
                    for f in range(FC):
                        last = pe.transpose(bank[5 + (m - 1) % 2][:, f * T:(f + 1) * T], gH[:, (m - 1) % 2, f * T:(f + 1) * T], ident)
                    last.then_inc(pe_hT, 1)
                if tile_in(k + 1):
                    tok_T(k + 1, (m + 1) % 4, ((k + 1) // 4 + 1) * 16)
                if tile_in(k - 2):
                    e = pe.value_load(eid[0:1, bass.ds(k - 2, 1)], min_val=0, max_val=E - 1)
                    pe.wait_ge(a_hh, k - 1)
                    pe.wait_ge(v_hl, k - 1)
                    at(pe, a_y, k - 2)
                    for f in range(FC):
                        w = bass.ds(e * WX + 2 * F + f * D, D)
                        fs = slice(f * T, (f + 1) * T)
                        last = split3(bank[7][:, 0:D], hTh[:, m % 2, fs], hTl[:, m % 2, fs], WH[:, w], WL[:, w],
                                      start=(f == 0), stop=(f == FC - 1))
                    last.then_inc(pe_y, 1)
            over_tiles(pe, step)


V_MB = 5 + 5 + 6 + 1
V_DP = V_MB + 1
V_BV = V_DP + 6 + 3 + 4 + 2 + 2


def kernel(**inputs):
    import numpy as _np
    import concourse.bacc as _bacc
    from concourse import mybir as _mybir
    from concourse.bass_utils import run_bass_kernel_spmd as _run

    a = {k: _np.asarray(v) for k, v in inputs.items()}
    p = _np.arange(T)
    const = _np.zeros((T, CONST), _np.float32)
    const[:, C_ID:C_ID + T] = p[:, None] == p[None, :]
    const[:, C_LT:C_LT + T] = p[:, None] < p[None, :]
    const[:, C_CM:C_CM + T] = _np.where(p[:, None] >= p[None, :], 0.0, -1e30)
    const[:, C_SL:C_SL + T] = p
    const[:, C_TL:C_TL + TT] = _np.arange(TT)
    const[:, C_LQ] = ((p % 32) // HD == 1) * HD ** -0.5
    const[:, C_LK] = (p % 32) // HD == 2
    const[:, C_EW:C_EW + E] = E - _np.arange(E)
    const[:, C_J:C_J + E] = T * _np.arange(E)
    kk = _np.repeat(_np.arange(2), B)
    const[:, C_PK:C_PK + 2 * B] = 2 * p[:, None] + kk[None, :] + 1
    const[:, C_TK:C_TK + 2 * B] = 2 * T * _np.tile(_np.arange(B), 2)
    const[:, C_ON:C_ON + 2] = 1.0
    wsmall = _np.concatenate([a[n].T for n in ("L0_xattn_Wq", "L0_xattn_Wk", "L0_xattn_Wv", "L0_xattn_Wo",
                                               "L0_ffn_shared_gate_up_w", "L0_ffn_shared_down_w", "L0_ffn_router_w")], axis=1)
    gu = a["L0_ffn_gate_up_w"].transpose(0, 2, 1)
    dn = a["L0_ffn_down_w"].transpose(0, 2, 1).reshape(E, FC, T, D).transpose(0, 2, 1, 3).reshape(E, T, FC * D)
    arrays = {
        "x": a["x"].reshape(B * T, D),
        "ctxT": a["ctx_1024"].reshape(B * T, D).T,
        "vec": _np.concatenate([a["L0_ffn_ln_gamma"], a["L0_ffn_ln_beta"], a["g_xattn"], a["g_ffn"]])[None, :],
        "wsmall": wsmall,
        "wexp": _np.concatenate([gu, dn], axis=2).reshape(E * D, WX),
        "const": const,
    }
    nc = _bacc.Bacc("TRN2", target_bir_lowering=False, num_devices=1)
    ins, args = {}, []
    for name, v in arrays.items():
        ins["in_" + name] = _np.ascontiguousarray(v)
        args.append(nc.dram_tensor("in_" + name, v.shape, _mybir.dt.from_np(v.dtype), kind="ExternalInput").ap())
    args.append(nc.dram_tensor("out", (B * T, D), _mybir.dt.float32, kind="ExternalOutput").ap())
    gated_layer(nc, *args)
    r = _run(nc, [ins], core_ids=[0])
    return r.results[0]["out"].reshape(B, T, D)
```

```python
import concourse.bass as bass
from concourse import mybir
from contextlib import ExitStack

B, T, D = 8, 128, 128
H, HD = 16, 8
SETS, ROWS = 4, 4
COPIES = 3
E, F = 8, 384
FC = F // T
SF = 128
PAIRS = 2 * B * T
TILES = PAIRS // T + E - 1
TT = TILES + 1
HALF = B * T // 2
UNITS = SETS * B
EPS = 1e-5
GU, DN = 2 * F, FC * D
CREDIT = 16
SKIP = 4096.0

WQ, WK, WV, WO, WSG, WSU, WSD, WR = 0, 128, 256, 384, 512, 640, 768, 896
WSMALL = WR + E
C_ID, C_LT, C_CM, C_SL, C_TL = 0, 128, 256, 384, 512
C_LQ, C_LK, C_EW, C_J, C_PK, C_TK, C_ON = 536, 537, 538, 546, 554, 570, 586
CONST = 588


def gated_layer(nc, x_h, ctxT_h, vec_h, wsmall_h, wgu_h, wdn_h, const_h, out_h):
    f32, f32r, bf16, i32 = mybir.dt.float32, mybir.dt.float32r, mybir.dt.bfloat16, mybir.dt.int32
    ALU, ACT, AX = mybir.AluOpType, mybir.ActivationFunctionType, mybir.AxisListType.X
    ctx = ExitStack()
    with ctx:
        def sb(name, shape, dt=f32):
            return ctx.enter_context(nc.sbuf_tensor(name, shape, dt))

        def sem(name):
            return ctx.enter_context(nc.semaphore(name))

        norm_d = nc.dram_tensor("norm_d", (B * T, D), f32, kind="Internal").ap()
        y_d = nc.dram_tensor("y_d", (PAIRS, D), f32, kind="Internal").ap()

        X = sb("X", [T, B * D])
        cT = sb("cT", [D, 2, T])
        vec = sb("vec", [T, 2 * D + 2])
        wsm = sb("wsm", [D, WSMALL])
        wstk = sb("wstk", [D, 2, SETS, 4 * 32])
        cst = sb("cst", [T, CONST])
        identb = sb("identb", [T, T], bf16)
        ltb = sb("ltb", [T, T], bf16)
        maskb = sb("maskb", [T, SETS, T], bf16)
        onesb = sb("onesb", [T, T], bf16)
        onesr = sb("onesr", [T, T], f32r)
        slotb = sb("slotb", [T, T], bf16)
        tg = sb("tg", [T, 2])
        st1 = sb("st1", [T, B, 6])
        mv1 = sb("mv1", [T, B, 2])
        ve1 = sb("ve1", [T, B])
        r1 = sb("r1", [T, B])
        mhalf = sb("mhalf", [T, B])
        xn = sb("xn", [T, 2, D])
        xT = sb("xT", [D, T])
        tq = sb("tq", [T, SETS, T], f32r)
        tk = sb("tk", [T, SETS, T], f32r)
        qS = sb("qS", [T, 2, SETS, T], f32r)
        kS = sb("kS", [T, 2, SETS, ROWS, T], f32r)
        V = sb("V", [T, 2, H, HD + 1])
        nm = sb("nm", [T, 4, SETS])
        R = sb("R", [T, 2, SETS, T], f32r)
        P = sb("P", [T, 4, SETS, T])
        rec = sb("rec", [T, H])
        att = sb("att", [T, D])
        aT = sb("aT", [D, T])
        X2 = sb("X2", [T, B * D])
        x2 = sb("x2", [T, 2, D])
        st2 = sb("st2", [T, 2, 6])
        mv2 = sb("mv2", [T, 2, 2])
        ve2 = sb("ve2", [T, 2])
        r2 = sb("r2", [T, 2])
        ng = sb("ng", [T, D])
        nr = sb("nr", [T, 2, D])
        NT = sb("NT", [D, B * T])
        wst = sb("wst", [D, 2, GU])
        WH = sb("WH", [D, E * GU], f32r)
        WL = sb("WL", [D, E * GU], f32r)
        WD = sb("WD", [D, E * DN])
        lg = sb("lg", [T, B, E])
        col = {n: sb("c_" + n, [T, B]) for n in ("mx", "sum", "rs", "p1", "w1", "p2", "w2", "dp", "e2", "o2", "g1", "g2")}
        ex = sb("ex", [T, B, E])
        pr = sb("pr", [T, B, E])
        eq = sb("eq", [T, 2, B, E])
        ew = sb("ew", [T, 2, B, E])
        M = sb("M", [T, 2, B, E])
        pr2 = sb("pr2", [T, B, E])
        Mb = sb("Mb", [T, B + 1, E], bf16)
        over = sb("over", [T, E, E])
        nt = sb("nt", [T, E])
        inc = sb("inc", [T, E])
        ts = sb("ts", [T, E])
        base = sb("base", [T, E])
        dest = sb("dest", [T, B, E])
        md = sb("md", [T, 2, B, E])
        slot = sb("slot", [T, 2, B])
        sloti = sb("sloti", [T, 2, B], i32)
        inti = sb("inti", [T, 2, 2, B], i32)
        intb = sb("intb", [T, 2 * B], bf16)
        Aoh = sb("Aoh", [T, 2 * B, T], bf16)
        tiles_of = sb("tiles_of", [T, 2 * B, TT])
        Bv = sb("Bv", [T, 2 * B, 2, TT], bf16)
        id1 = sb("id1", [T, TT])
        none = sb("none", [T, TT])
        gi = sb("gi", [T, TT])
        si = sb("si", [T, TT])
        gidx = sb("gidx", [T, TT], i32)
        gtok = sb("gtok", [T, TT], i32)
        sidx = sb("sidx", [T, TT], i32)
        gring = sb("gring", [T, 4], i32)
        sring = sb("sring", [T, 2], i32)
        cmpe = sb("cmpe", [1, TT, E])
        eidf = sb("eidf", [1, TT])
        goff = sb("goff", [1, TT], i32)
        doff = sb("doff", [1, TT], i32)
        sS = sb("sS", [SF, B * T])
        sH = sb("sH", [SF, B * T])
        XG = sb("XG", [T, 4, D])
        gTh = sb("gTh", [D, 2, T], f32r)
        gTl = sb("gTl", [D, 2, T], f32r)
        gS = sb("gS", [T, 2, F])
        gH = sb("gH", [T, 2, F])
        hT = sb("hT", [T, 2, F])
        Y = sb("Y", [T, 2, D])
        YG = sb("YG", [T, B, 2, D])
        out_sb = sb("out_sb", [T, B, D])

        bank = [ctx.enter_context(nc.psum_tensor(f"bank{n}", [128, 512], f32)) for n in range(8)]
        Sb, Tb, Ob, Qb, Kb, Mi = bank[0:2], bank[2:4], bank[4], bank[5], bank[6], bank[7]

        def sems(name, n):
            return [sem(f"{name}{m}") for m in range(n)]

        ld_small, ld_const, ld_vec, ld_d = (sem("ld_" + n) for n in ("small", "const", "vec", "d"))
        ld_x, ld_c, ld_w, st_n, ld_y = (sems(n, 2) for n in ("ld_x", "ld_c", "ld_w", "st_n", "ld_y"))
        pe_S, pe_T, pe_PV, v_max, p_R, p_mask, a_exp = (
            sems(n, SETS) for n in ("pe_S", "pe_T", "pe_PV", "v_max", "p_R", "p_mask", "a_exp"))
        pe_xT, pe_q, pe_k, pe_v, pe_aT, pe_wo, pe_nT = (sem("pe_" + n) for n in ("xT", "q", "k", "v", "aT", "wo", "nT"))
        v_xn, v_q, v_k, v_rec, v_att, v_x2, v_st2, v_mv2, v_ve2, v_ng, v_n, v_wl = (
            sem("v_" + n) for n in ("xn", "q", "k", "rec", "att", "x2", "st2", "mv2", "ve2", "ng", "n", "wl"))
        a_xT, a_tq, a_tk, a_v, a_aT, a_nT, a_x2, a_wh = (
            sem("a_" + n) for n in ("xT", "tq", "tk", "v", "aT", "nT", "x2", "wh"))
        p_r2 = sem("p_r2")
        v_setup, v_st1, v_ve1, p_set, p_r1, a_tg = (sem(n) for n in ("v_setup", "v_st1", "v_ve1", "p_set", "p_r1", "a_tg"))
        pe_lg, pe_rank, pe_tab, v_rt, a_ex, a_e2, v_ready = (
            sem(n) for n in ("pe_lg", "pe_rank", "pe_tab", "v_rt", "a_ex", "a_e2", "v_ready"))
        pe_sgu, pe_sy, a_ss, v_sh, v_x3 = (sem(n) for n in ("pe_sgu", "pe_sy", "a_ss", "v_sh", "v_x3"))
        gat, sca, pe_gT, pe_gu, pe_hT, pe_y, a_gh, v_gl, a_s, v_h, a_hT, a_y, v_gi, v_si = (
            sems(n, 4) for n in ("gat", "sca", "pe_gT", "pe_gu", "pe_hT", "pe_y", "a_gh", "v_gl", "a_s", "v_h", "a_hT", "a_y",
                                 "v_gi", "v_si"))
        p_go, v_go = sem("p_go"), sem("v_go")
        v_f1, v_out, st_o = sem("v_f1"), sem("v_out"), sem("st_o")

        block = ctx.enter_context(nc.Block())

        def done(eng, list_, n, m, by=1):
            q, m = divmod(m, 4)
            if not isinstance(n, int) or n + q >= 0:
                eng.wait_ge(list_[m], (n + (q + 1)) * by)

        def unit_done(eng, list_, i, w):
            q, m = divmod(w, SETS)
            if not isinstance(i, int) or i + q >= 0:
                eng.wait_ge(list_[m], i + (q + 1))

        def seq_done(eng, s, i, c):
            if not isinstance(i, int) or i + c >= 0:
                eng.wait_ge(s, i + (c + 1))

        def load_done(eng, list_, i, c):
            q, m = divmod(c, 2)
            eng.wait_ge(list_[m], i * 8 + 16 * (q + 1))

        def has(i, c):
            return not isinstance(i, int) or 0 <= i + c < B

        def seq(b):
            return bass.ds(b * T, T)

        def over_pairs(eng, body):
            body(0)
            with eng.Fori(2, B - 3, 2) as i:
                body(i)
            body(B - 2)

        def over_tiles(eng, step):
            last = (TILES - 3) // 4
            for m in range(4):
                step(0, m)
            with eng.Fori(1, last) as n:
                for m in range(4):
                    step(n, m)
            for k in range(4 * last, TILES + 2):
                step(k // 4, k % 4)

        def tile_in(n, m):
            return not isinstance(n, int) or 0 <= 4 * n + m < TILES

        @block.sync
        def _(sp):
            def load_x(h):
                bs = slice(h * B // 2, (h + 1) * B // 2)
                sp.dma_start(X[:, :].rearrange("p (b d) -> p b d", b=B)[:, bs, :],
                             x_h.rearrange("(b p) d -> p b d", b=B)[:, bs, :]).then_inc(ld_x[h], 16)

            def load_c(b, c):
                sp.dma_start(cT[:, c, :], ctxT_h[:, seq(b)]).then_inc(ld_c[c], 16)

            def load_w(e, c):
                sp.dma_start(wst[:, c, :], wgu_h[bass.ds(e * D, D), :]).then_inc(ld_w[c], 16)

            for c in range(2):
                sp.sem_inc(st_n[c], CREDIT)
            load_x(0)
            load_x(1)
            sp.dma_start(wsm[:, :], wsmall_h).then_inc(ld_small, 16)
            sp.dma_start(cst[:, :], const_h).then_inc(ld_const, 16)
            load_c(0, 0)
            load_c(1, 1)
            sp.dma_start(vec[:, :], vec_h.to_broadcast((T, 2 * D + 2))).then_inc(ld_vec, 16)
            load_w(0, 0)
            load_w(1, 1)
            sp.dma_start(WD[:, :], wdn_h).then_inc(ld_d, 16)

            def pair(i):
                for c in range(2):
                    b = i + c
                    if has(i, c + 2):
                        seq_done(sp, pe_v, i, c)
                        load_c(b + 2, c)
                    if has(i, c - 2):
                        seq_done(sp, v_n, i, c - 2)
                        sp.dma_start(norm_d[seq(b - 2), :], nr[:, c, :]).then_inc(st_n[c], 16)
                    if has(i, c + 2):
                        seq_done(sp, a_wh, i, c)
                        seq_done(sp, v_wl, i, c)
                        load_w(b + 2, c)
            over_pairs(sp, pair)
            for c in range(2):
                seq_done(sp, v_n, B - 2, c)
                sp.dma_start(norm_d[seq(B - 2 + c), :], nr[:, c, :]).then_inc(st_n[c], 16)
            for m in range(4):
                sp.wait_ge(sca[m], 16 * len(range(m, TILES, 4)))
            yv = y_d.rearrange("(b p k) d -> p b (k d)", b=B, k=2)
            for h in range(2):
                bs = slice(h * B // 2, (h + 1) * B // 2)
                sp.dma_start(YG[:, bs, :, :].rearrange("p b k d -> p b (k d)"), yv[:, bs, :]).then_inc(ld_y[h], 16)
            for h in range(2):
                bs = slice(h * B // 2, (h + 1) * B // 2)
                sp.wait_ge(v_out, (h + 1) * B // 2)
                sp.dma_start(out_h.rearrange("(b p) d -> p b d", b=B)[:, bs, :], out_sb[:, bs, :]).then_inc(st_o, 16)
            sp.wait_ge(st_o, 32)

        @block.gpsimd
        def _(pool):
            pool.memset(mhalf[:, :], -0.5).then_inc(p_set, 1)
            for c in range(2):
                pool.memset(kS[:, c].bitcast(f32), 0.0).then_inc(p_set, 1)
            pool.memset(V[:, :, :, HD:HD + 1], 1.0).then_inc(p_set, 1)
            pool.memset(Mb[:, B, :], 0.0).then_inc(p_set, 1)
            pool.wait_ge(p_set, 1)
            pool.wait_ge(v_ve1, 1)
            pool.tensor_tensor(r1[:, :], ve1[:, :], mhalf[:, :], ALU.pow).then_inc(p_r1, 1)

            def diag(i, w):
                unit_done(pool, v_max, i, w)
                unit_done(pool, pe_T, i, w - 2)
                pool.sem_inc(p_go, 1)
                pool.affine_select(out=R[:, w % 2], in_=nm[:, w % 4, :].unsqueeze(2).to_broadcast((T, ROWS, T)),
                                   pattern=[[0, ROWS], [-1, T]], compare_op=ALU.is_equal, fill=0.0, base=0,
                                   channel_multiplier=1).then_inc(p_R[w % 4], 1)

            def causal(i, w):
                unit_done(pool, a_exp, i, w)
                pool.sem_inc(p_go, 1)
                pool.affine_select(out=P[:, w % 4], in_=P[:, w % 4], pattern=[[0, ROWS], [1, T]],
                                   compare_op=ALU.is_ge, fill=0.0, base=0, channel_multiplier=-1).then_inc(p_mask[w % 4], 1)

            def rstd2(i, c):
                seq_done(pool, v_ve2, i, c)
                pool.tensor_tensor(r2[:, c % 2:c % 2 + 1], ve2[:, c % 2:c % 2 + 1], mhalf[:, 0:1], ALU.pow).then_inc(p_r2, 1)

            diag(0, 0)

            def pair(i):
                for w in range(8):
                    c, s = divmod(w, SETS)
                    if has(i, (w + 1) // SETS):
                        diag(i, w + 1)
                    if not isinstance(i, int) or 4 * i + w >= 1:
                        causal(i, w - 1)
                    if s == 0 and has(i, c - 2):
                        rstd2(i, c - 2)
            over_pairs(pool, pair)
            causal(B - 2, 7)
            rstd2(B - 2, 0)
            rstd2(B - 2, 1)

            pool.wait_ge(v_ready, 1)
            for c in range(2):
                pool.wait_ge(st_n[c], CREDIT + 16 * B // 2)

            def gather(n, m):
                done(pool, v_gi, n, m)
                done(pool, pe_gT, n, m - 4)
                pool.sem_inc(p_go, 1)
                pool.indirect_dma_start(XG[:, m % 4, :], None, norm_d, bass.IndirectOffsetOnAxis(gring[:, m % 4:m % 4 + 1], 0),
                                        bounds_check=B * T - 1, oob_is_err=False).then_inc(gat[m % 4], 16)

            def scatter(n, m):
                done(pool, v_si, n, m)
                done(pool, a_y, n, m)
                pool.sem_inc(p_go, 1)
                pool.indirect_dma_start(y_d, bass.IndirectOffsetOnAxis(sring[:, m % 2:m % 2 + 1], 0), Y[:, m % 2, :], None,
                                        bounds_check=PAIRS - 1, oob_is_err=False).then_inc(sca[m % 4], 16)
            for m in range(3):
                gather(0, m)

            def step(n, m):
                if tile_in(n, m + 3):
                    gather(n, m + 3)
                if tile_in(n, m - 2):
                    scatter(n, m - 2)
            over_tiles(pool, step)

        @block.scalar
        def _(act):
            act.wait_ge(ld_vec, 16)
            act.activation(tg[:, :], vec[:, 2 * D:2 * D + 2], ACT.Tanh).then_inc(a_tg, 1)
            act.wait_ge(ld_const, 16)

            def x_out(i, c):
                seq_done(act, pe_xT, i, c)
                seq_done(act, pe_q, i, c - 1)
                act.activation(xT[:, :], Mi[:, 0:T], ACT.Copy).then_inc(a_xT, 1)

            def qkv(i, c):
                seq_done(act, pe_q, i, c)
                seq_done(act, v_q, i, c - 1)
                act.activation(tq[:, :, :], Qb[:, :].rearrange("p (s t) -> p s t", s=SETS), ACT.Copy,
                               scale=cst[:, C_LQ:C_LQ + 1]).then_inc(a_tq, 1)
                seq_done(act, pe_k, i, c)
                seq_done(act, v_k, i, c - 1)
                act.activation(tk[:, :, :], Kb[:, :].rearrange("p (s t) -> p s t", s=SETS), ACT.Copy,
                               scale=cst[:, C_LK:C_LK + 1]).then_inc(a_tk, 1)
                seq_done(act, pe_v, i, c)
                unit_done(act, pe_PV, i, SETS * (c - 1) - 1)
                act.activation(V[:, c % 2, :, 0:HD], Mi[:, 0:D].rearrange("p (h e) -> p h e", h=H), ACT.Copy)\
                   .then_inc(a_v, 1)

            def expo(i, w):
                unit_done(act, pe_T, i, w)
                unit_done(act, pe_PV, i, w - 4)
                act.activation(P[:, w % 4], Tb[w % 2][:, :].rearrange("p (j t) -> p j t", j=ROWS), ACT.Exp,
                               scale=HD ** -0.5).then_inc(a_exp[w % 4], 1)

            def att_out(i, c):
                seq_done(act, pe_aT, i, c)
                seq_done(act, pe_wo, i, c - 1)
                act.activation(aT[:, :], Mi[:, 0:T], ACT.Copy).then_inc(a_aT, 1)

            def keep(i, c):
                seq_done(act, v_x2, i, c)
                act.activation(X2[:, seq(i + c)], x2[:, c % 2, :], ACT.Copy).then_inc(a_x2, 1)

            def n_out(i, c):
                seq_done(act, pe_nT, i, c)
                act.activation(NT[:, seq(i + c)], Qb[:, 0:T], ACT.Copy).then_inc(a_nT, 1)

            def w_hi(i, c):
                load_done(act, ld_w, i, c)
                act.activation(WH[:, bass.ds((i + c) * GU, GU)], wst[:, c, :], ACT.Copy).then_inc(a_wh, 1)

            x_out(0, 0)
            qkv(0, 0)

            def pair(i):
                for w in range(8):
                    c, s = divmod(w, SETS)
                    if s == 0 and has(i, c + 1):
                        x_out(i, c + 1)
                    if s == 1 and has(i, c + 1):
                        qkv(i, c + 1)
                    if s == 2 and has(i, c - 2):
                        keep(i, c - 2)
                    if s == 3 and has(i, c - 1):
                        att_out(i, c - 1)
                    if s == 3 and has(i, c - 2):
                        n_out(i, c - 2)
                    expo(i, w)
                    if s == 2:
                        w_hi(i, c)
            over_pairs(act, pair)
            last = B - 2
            att_out(last, 1)
            keep(last, 0)
            n_out(last, 0)
            keep(last, 1)
            n_out(last, 1)

            act.wait_ge(v_rt, 2)
            act.activation(ex[:, :, :], lg[:, :, :], ACT.Exp).then_inc(a_ex, 1)
            act.wait_ge(v_rt, V_DP)
            act.activation(col["e2"][:, :], col["dp"][:, :], ACT.Exp).then_inc(a_e2, 1)

            for h in range(2):
                act.wait_ge(pe_sgu, 2 * h + 1)
                act.activation(sS[:, h * HALF:(h + 1) * HALF], bank[3 + h][:, :], ACT.Silu).then_inc(a_ss, 1)

            def tok_hi(n, m):
                done(act, pe_gT, n, m)
                done(act, pe_gu, n, m - 2)
                act.activation(gTh[:, m % 2, :], bank[4][:, 0:T], ACT.Copy).then_inc(a_gh[m % 4], 1)

            tok_hi(0, 0)

            def step(n, m):
                if tile_in(n, m - 1):
                    done(act, pe_hT, n, m - 1)
                    done(act, pe_y, n, m - 3)
                    act.activation(hT[:, (m - 1) % 2, :], bank[5 + (m - 1) % 2][:, 0:F], ACT.Copy).then_inc(a_hT[(m - 1) % 4], 1)
                if tile_in(n, m + 1):
                    tok_hi(n, m + 1)
                if tile_in(n, m - 2):
                    done(act, pe_y, n, m - 2)
                    done(act, sca, n, m - 4, 16)
                    act.activation(Y[:, m % 2, :], bank[7][:, 0:D], ACT.Copy).then_inc(a_y[(m - 2) % 4], 1)
                if tile_in(n, m):
                    done(act, pe_gu, n, m)
                    done(act, v_h, n, m - 2)
                    act.activation(gS[:, m % 2, :], bank[m % 2][:, 0:F], ACT.Silu).then_inc(a_s[m % 4], 1)
            over_tiles(act, step)

        @block.vector
        def _(dve):
            for h in range(2):
                dve.wait_ge(ld_x[h], 16)
                for b in range(h * B // 2, (h + 1) * B // 2):
                    dve.bn_stats(st1[:, b, :], X[:, b * D:(b + 1) * D]).then_inc(v_st1, 1)
            for b in range(B):
                dve.wait_ge(v_st1, b + 1)
                dve.bn_aggr(mv1[:, b, :], st1[:, b, :]).then_inc(v_st1, 1)
            dve.wait_ge(v_st1, 2 * B)
            dve.tensor_scalar(ve1[:, :], mv1[:, :, 1], EPS, None, ALU.add).then_inc(v_ve1, 1)
            for n in range(2):
                dve.memset(wstk[:, n], 0.0).then_inc(v_setup, 1)
            dve.wait_ge(ld_small, 16)
            dve.wait_ge(v_setup, 2)
            for n, o in ((0, WQ), (1, WK)):
                for r in range(COPIES):
                    d = wstk[:, n].rearrange("p s (j r e) -> p (s j) r e", j=ROWS, e=HD)
                    dve.tensor_copy(d[:, :, r, :], wsm[:, o:o + D].rearrange("p (h e) -> p h e", e=HD)).then_inc(v_setup, 1)
            dve.wait_ge(ld_const, 16)
            for dst, src in ((identb[:, :], C_ID), (ltb[:, :], C_LT), (slotb[:, :], C_SL)):
                dve.tensor_copy(dst, cst[:, src:src + T]).then_inc(v_setup, 1)
            dve.tensor_copy(maskb[:, :, :], cst[:, C_CM:C_CM + T].unsqueeze(1).to_broadcast((T, SETS, T))).then_inc(v_setup, 1)
            dve.tensor_copy(onesr[:, :], cst[:, C_ON:C_ON + 1].to_broadcast((T, T))).then_inc(v_setup, 1)
            dve.tensor_copy(onesb[:, :], cst[:, C_ON:C_ON + 1].to_broadcast((T, T))).then_inc(v_setup, 1)

            def normalise(i, c):
                seq_done(dve, pe_xT, i, c - 2)
                b = i + c
                dve.tensor_scalar(xn[:, c % 2, :], X[:, seq(b)], mv1[:, bass.ds(b, 1), 0], r1[:, bass.ds(b, 1)],
                                  ALU.subtract, ALU.mult).then_inc(v_xn, 1)

            def stack(i, c):
                seq_done(dve, a_tq, i, c)
                unit_done(dve, pe_T, i, SETS * (c - 1) - 1)
                dve.tensor_tensor(qS[:, c % 2], Qb[:, :].rearrange("p (s t) -> p s t", s=SETS), tq[:, :, :].bitcast(f32),
                                  ALU.subtract).then_inc(v_q, 1)
                seq_done(dve, a_tk, i, c)
                for j in range(ROWS):
                    r = slice(32 * j, 32 * j + 32)
                    last = dve.tensor_tensor(kS[r, c % 2, :, j, :], Kb[r, :].rearrange("p (s t) -> p s t", s=SETS),
                                             tk[r, :, :].bitcast(f32), ALU.subtract)
                last.then_inc(v_k, 1)

            def negmax(i, w):
                unit_done(dve, pe_S, i, w)
                unit_done(dve, p_R, i, w - 4)
                dve.tensor_reduce(nm[:, w % 4, :], Sb[w % 2][:, :].rearrange("p (j t) -> p j t", j=ROWS), AX, ALU.max,
                                  negate=True).then_inc(v_max[w % 4], 1)

            def weigh(i, c):
                o = Ob[:, 0:H * (HD + 1)].rearrange("p (h e) -> p h e", h=H)
                unit_done(dve, pe_PV, i, SETS * c + SETS - 1)
                dve.reciprocal(rec[:, :], o[:, :, HD]).then_inc(v_rec, 1)
                seq_done(dve, v_rec, i, c)
                seq_done(dve, pe_aT, i, c - 1)
                dve.tensor_tensor(att[:, :].rearrange("p (h e) -> p h e", h=H), o[:, :, 0:HD],
                                  rec[:, :].unsqueeze(2).to_broadcast((T, H, HD)), ALU.mult).then_inc(v_att, 1)

            def residual(i, c):
                b = i + c
                seq_done(dve, pe_wo, i, c)
                dve.scalar_tensor_tensor(x2[:, c % 2, :], Mi[:, 0:D], tg[:, 0:1], X[:, seq(b)], ALU.mult,
                                         ALU.add).then_inc(v_x2, 1)
                seq_done(dve, v_x2, i, c)
                dve.bn_stats(st2[:, c % 2, :], x2[:, c % 2, :]).then_inc(v_st2, 1)
                seq_done(dve, v_st2, i, c)
                dve.sem_inc(v_go, 1)
                dve.bn_aggr(mv2[:, c % 2, :], st2[:, c % 2, :]).then_inc(v_mv2, 1)
                seq_done(dve, v_mv2, i, c)
                dve.tensor_scalar(ve2[:, c % 2:c % 2 + 1], mv2[:, c % 2, 1:2], 1.0 + EPS, EPS * EPS, ALU.mult,
                                  ALU.add).then_inc(v_ve2, 1)

            def normed(i, c):
                q, m = divmod(c, 2)
                dve.wait_ge(st_n[m], i * 8 + 16 * (q + 1))
                dve.scalar_tensor_tensor(ng[:, :], x2[:, c % 2, :], mv2[:, c % 2, 0:1], vec[:, 0:D], ALU.subtract,
                                         ALU.mult).then_inc(v_ng, 1)
                seq_done(dve, v_ng, i, c)
                seq_done(dve, p_r2, i, c)
                dve.scalar_tensor_tensor(nr[:, c % 2, :], ng[:, :], r2[:, c % 2:c % 2 + 1], vec[:, D:2 * D], ALU.mult,
                                         ALU.add).then_inc(v_n, 1)

            def w_lo(i, c):
                e = bass.ds((i + c) * GU, GU)
                seq_done(dve, a_wh, i, c)
                dve.tensor_tensor(WL[:, e], wst[:, c, :], WH[:, e].bitcast(f32), ALU.subtract).then_inc(v_wl, 1)

            dve.wait_ge(p_r1, 1)
            normalise(0, 0)
            normalise(0, 1)
            dve.wait_ge(p_set, 3)
            stack(0, 0)
            dve.wait_ge(a_tg, 1)
            negmax(0, 0)

            def pair(i):
                for w in range(8):
                    c, s = divmod(w, SETS)
                    if has(i, (w + 1) // SETS):
                        negmax(i, w + 1)
                    if s == 0 and has(i, c - 2):
                        residual(i, c - 2)
                    if s == 1 and has(i, c + 1):
                        stack(i, c + 1)
                    if s == 1 and has(i, c - 2):
                        normed(i, c - 2)
                    if s == 2 and has(i, c - 1):
                        weigh(i, c - 1)
                    if s == 2 and has(i, c + 2):
                        normalise(i, c + 2)
                    if s == 3:
                        w_lo(i, c)
            over_pairs(dve, pair)
            last = B - 2
            residual(last, 0)
            weigh(last, 1)
            normed(last, 0)
            residual(last, 1)
            normed(last, 1)

            steps = [0]

            def link(ins):
                steps[0] += 1
                ins.then_inc(v_rt, 1)
                dve.wait_ge(v_rt, steps[0])

            def wide(a):
                return a.unsqueeze(2).to_broadcast((T, B, E))

            lgp = bank[0][:, 0:B * E].rearrange("p (b e) -> p b e", b=B)
            dve.wait_ge(pe_lg, 1)
            link(dve.tensor_reduce(col["mx"][:, :], lgp, AX, ALU.max))
            link(dve.tensor_tensor(lg[:, :, :], lgp, wide(col["mx"][:, :]), ALU.subtract))
            dve.wait_ge(a_ex, 1)
            link(dve.tensor_reduce(col["sum"][:, :], ex[:, :, :], AX, ALU.add))
            link(dve.reciprocal(col["rs"][:, :], col["sum"][:, :]))
            link(dve.tensor_tensor(pr[:, :, :], ex[:, :, :], wide(col["rs"][:, :]), ALU.mult))
            for n, src in ((0, pr), (1, pr2)):
                p, wn = col[f"p{n + 1}"], col[f"w{n + 1}"]
                if n:
                    link(dve.scalar_tensor_tensor(pr2[:, :, :], M[:, 0], -2.0, pr[:, :, :], ALU.mult, ALU.add))
                link(dve.tensor_reduce(p[:, :], src[:, :, :], AX, ALU.max))
                link(dve.tensor_tensor(eq[:, n], src[:, :, :], wide(p[:, :]), ALU.is_equal))
                link(dve.tensor_tensor(ew[:, n], eq[:, n], cst[:, C_EW:C_EW + E].unsqueeze(1).to_broadcast((T, B, E)), ALU.mult))
                link(dve.tensor_reduce(wn[:, :], ew[:, n], AX, ALU.max))
                link(dve.tensor_tensor(M[:, n], ew[:, n], wide(wn[:, :]), ALU.is_equal))
            dve.wait_ge(p_set, 3)
            link(dve.tensor_tensor(Mb[:, 0:B, :], M[:, 0], M[:, 1], ALU.add))
            assert steps[0] == V_MB
            link(dve.tensor_tensor(col["dp"][:, :], col["p2"][:, :], col["p1"][:, :], ALU.subtract))
            assert steps[0] == V_DP
            dve.wait_ge(pe_rank, 1)
            rank = bank[1][:, 0:(B + 1) * E].rearrange("p (b e) -> p b e", e=E)
            link(dve.tensor_tensor(over[:, :, :], rank[:, B, :].unsqueeze(2).to_broadcast((T, E, E)),
                                   cst[:, C_J:C_J + E].unsqueeze(1).to_broadcast((T, E, E)), ALU.is_gt))
            link(dve.tensor_reduce(nt[:, :], over[:, :, :], AX, ALU.add))
            link(dve.tensor_tensor_scan(inc[:, :], cst[:, C_ON:C_ON + 1].to_broadcast((T, E)), nt[:, :], 0.0, ALU.mult, ALU.add))
            link(dve.tensor_tensor(ts[:, :], inc[:, :], nt[:, :], ALU.subtract))
            link(dve.tensor_scalar(base[:, :], ts[:, :], float(T), None, ALU.mult))
            link(dve.tensor_tensor(dest[:, :, :], rank[:, 0:B, :], base[:, :].unsqueeze(1).to_broadcast((T, B, E)), ALU.add))
            for n in range(2):
                link(dve.tensor_tensor(md[:, n], M[:, n], dest[:, :, :], ALU.mult))
            link(dve.tensor_reduce(slot[:, :, :], md[:, :, :, :], AX, ALU.add))
            link(dve.tensor_copy(sloti[:, :, :], slot[:, :, :]))
            link(dve.tensor_scalar(inti[:, 0], sloti[:, :, :], T - 1, None, ALU.bitwise_and))
            link(dve.tensor_scalar(inti[:, 1], sloti[:, :, :], T.bit_length() - 1, None, ALU.arith_shift_right))
            link(dve.tensor_copy(intb[:, :], inti[:, 0].rearrange("p k b -> p (k b)")))
            link(dve.tensor_tensor(Aoh[:, :, :], slotb[:, :].unsqueeze(1).to_broadcast((T, 2 * B, T)),
                                   intb[:, :].unsqueeze(2).to_broadcast((T, 2 * B, T)), ALU.is_equal))
            link(dve.tensor_tensor(tiles_of[:, :, :], cst[:, C_TL:C_TL + TT].unsqueeze(1).to_broadcast((T, 2 * B, TT)),
                                   inti[:, 1].rearrange("p k b -> p (k b)").unsqueeze(2).to_broadcast((T, 2 * B, TT)), ALU.is_equal))
            for n, o in ((0, C_PK), (1, C_TK)):
                link(dve.tensor_tensor(Bv[:, :, n, :], tiles_of[:, :, :],
                                       cst[:, o:o + 2 * B].unsqueeze(2).to_broadcast((T, 2 * B, TT)), ALU.mult))
            assert steps[0] == V_BV
            link(dve.tensor_tensor(cmpe[:, :, 0:E - 1], cst[0:1, C_TL:C_TL + TT].unsqueeze(2).to_broadcast((1, TT, E - 1)),
                                   ts[0:1, 1:E].unsqueeze(1).to_broadcast((1, TT, E - 1)), ALU.is_ge))
            link(dve.tensor_reduce(eidf[:, :], cmpe[:, :, 0:E - 1], AX, ALU.add))
            link(dve.tensor_scalar(goff[:, :], eidf[:, :], float(GU), None, ALU.mult))
            link(dve.tensor_scalar(doff[:, :], eidf[:, :], float(DN), None, ALU.mult))
            dve.wait_ge(a_e2, 1)
            link(dve.tensor_scalar(col["o2"][:, :], col["e2"][:, :], 1.0, None, ALU.add))
            link(dve.reciprocal(col["g1"][:, :], col["o2"][:, :]))
            link(dve.tensor_tensor(col["g2"][:, :], col["e2"][:, :], col["g1"][:, :], ALU.mult))
            dve.wait_ge(pe_tab, 1)
            tab = bank[2][:, 0:2 * TT].rearrange("p (n i) -> p n i", n=2)
            link(dve.tensor_reduce(id1[:, :], tab.rearrange("p n i -> p i n"), AX, ALU.add))
            link(dve.tensor_scalar(gi[:, :], id1[:, :], -1.0, 0.0, ALU.add, ALU.max))
            link(dve.tensor_copy(gidx[:, :], gi[:, :]))
            link(dve.tensor_scalar(gtok[:, :], gidx[:, :], 1, None, ALU.arith_shift_right))
            link(dve.tensor_scalar(none[:, :], id1[:, :], 0.0, SKIP, ALU.is_equal, ALU.mult))
            link(dve.tensor_tensor(si[:, :], gi[:, :], none[:, :], ALU.add))
            dve.tensor_copy(sidx[:, :], si[:, :]).then_inc(v_ready, 1)

            for h in range(2):
                hs = slice(h * HALF, (h + 1) * HALF)
                dve.wait_ge(a_ss, h + 1)
                dve.wait_ge(pe_sgu, 2 * h + 2)
                dve.tensor_tensor(sH[:, hs], sS[:, hs], bank[5 + h][:, :], ALU.mult).then_inc(v_sh, 1)
            for h in range(2):
                hs = slice(h * HALF, (h + 1) * HALF)
                dve.wait_ge(pe_sy, h + 1)
                dve.scalar_tensor_tensor(X2[:, hs], bank[h][:, :], tg[:, 1:2], X2[:, hs], ALU.mult, ALU.add).then_inc(v_x3, 1)

            def tok_lo(n, m):
                done(dve, a_gh, n, m)
                done(dve, pe_gu, n, m - 2)
                dve.tensor_tensor(gTl[:, m % 2, :], bank[4][:, 0:T], gTh[:, m % 2, :].bitcast(f32),
                                  ALU.subtract).then_inc(v_gl[m % 4], 1)

            def in_indices(n, m):
                done(dve, gat, n, m - 4, 16)
                dve.tensor_copy(gring[:, m % 4:m % 4 + 1], gtok[:, bass.ds(4 * n + m, 1)]).then_inc(v_gi[m % 4], 1)

            def out_indices(n, m):
                done(dve, sca, n, m - 2, 16)
                dve.tensor_copy(sring[:, m % 2:m % 2 + 1], sidx[:, bass.ds(4 * n + m, 1)]).then_inc(v_si[m % 4], 1)

            for m in range(3):
                in_indices(0, m)
            tok_lo(0, 0)

            def step(n, m):
                if tile_in(n, m + 3):
                    in_indices(n, m + 3)
                if tile_in(n, m - 2):
                    out_indices(n, m - 2)
                if tile_in(n, m + 1):
                    tok_lo(n, m + 1)
                if tile_in(n, m):
                    done(dve, a_s, n, m)
                    done(dve, pe_hT, n, m - 2)
                    dve.tensor_tensor(gH[:, m % 2, :], gS[:, m % 2, :], bank[2 + m % 2][:, 0:F], ALU.mult).then_inc(v_h[m % 4], 1)
            over_tiles(dve, step)

            dve.wait_ge(v_rt, steps[0])
            for h in range(2):
                dve.wait_ge(ld_y[h], 16)
                bs = range(h * B // 2, (h + 1) * B // 2)
                for k in range(2):
                    for b in bs:
                        dve.tensor_scalar(YG[:, b, k, :], YG[:, b, k, :], col[f"g{k + 1}"][:, b:b + 1], tg[:, 1:2], ALU.mult,
                                          ALU.mult).then_inc(v_f1, 1)
                dve.wait_ge(v_f1, h * (B + 1) + B)
                dve.tensor_tensor(YG[:, bs[0]:bs[-1] + 1, 0, :], YG[:, bs[0]:bs[-1] + 1, 0, :],
                                  YG[:, bs[0]:bs[-1] + 1, 1, :], ALU.add).then_inc(v_f1, 1)
                dve.wait_ge(v_f1, (h + 1) * (B + 1))
                for b in bs:
                    dve.tensor_tensor(out_sb[:, b, :], YG[:, b, 0, :], X2[:, b * D:(b + 1) * D], ALU.add).then_inc(v_out, 1)

        @block.tensor
        def _(pe):
            ident = cst[:, C_ID:C_ID + T]

            def x_T(i, c):
                seq_done(pe, v_xn, i, c)
                seq_done(pe, a_v, i, c - 1)
                seq_done(pe, v_x2, i, c - 3)
                pe.transpose(Mi[:, 0:T], xn[:, c % 2, :], ident).then_inc(pe_xT, 1)

            def qkv(i, c):
                seq_done(pe, a_xT, i, c)
                for s in range(SETS):
                    last = pe.matmul(Qb[:, s * T:(s + 1) * T], wstk[:, 0, s, :], xT[:, :], start=True, stop=True)
                last.then_inc(pe_q, 1)
                load_done(pe, ld_c, i, c)
                seq_done(pe, v_k, i, c - 1)
                for s in range(SETS):
                    last = pe.matmul(Kb[:, s * T:(s + 1) * T], wstk[:, 1, s, :], cT[:, c % 2, :], start=True, stop=True)
                last.then_inc(pe_k, 1)
                pe.matmul(Mi[:, 0:D], cT[:, c % 2, :], wsm[:, WV:WV + D], start=True, stop=True).then_inc(pe_v, 1)

            def scores(i, w):
                c, s = divmod(w, SETS)
                if s == 0:
                    seq_done(pe, v_q, i, c)
                    seq_done(pe, v_k, i, c)
                unit_done(pe, v_max, i, w - 2)
                pe.matmul(Sb[w % 2][:, :], identb[:, :], maskb[:, :, :].rearrange("p s t -> p (s t)"), start=True, stop=False)
                pe.matmul(Sb[w % 2][:, :], qS[:, c % 2, s, :], kS[:, c % 2, s].rearrange("p j t -> p (j t)"), start=False,
                          stop=True).then_inc(pe_S[w % 4], 1)

            def scores_T(i, w):
                c, s = divmod(w, SETS)
                unit_done(pe, a_exp, i, w - 2)
                for j in range(ROWS):
                    pe.matmul(Tb[w % 2][:, j * T:(j + 1) * T], kS[:, c % 2, s, j, :], qS[:, c % 2, s, :], start=(j == 0), stop=False)
                unit_done(pe, p_R, i, w)
                pe.matmul(Tb[w % 2][:, :], onesr[:, :], R[:, w % 2].rearrange("p j t -> p (j t)"), start=False,
                          stop=True).then_inc(pe_T[w % 4], 1)

            def values(i, w):
                c, s = divmod(w, SETS)
                unit_done(pe, p_mask, i, w)
                if s == 0:
                    seq_done(pe, a_v, i, c)
                    seq_done(pe, v_att, i, c - 1)
                for j in range(ROWS):
                    h = ROWS * s + j
                    last = pe.matmul(Ob[:, h * (HD + 1):(h + 1) * (HD + 1)], P[:, w % 4, j, :], V[:, c % 2, h, :],
                                     start=(s == 0 and j == 0), stop=(s == SETS - 1 and j == ROWS - 1))
                last.then_inc(pe_PV[w % 4], 1)

            def att_T(i, c):
                seq_done(pe, v_att, i, c)
                pe.transpose(Mi[:, 0:T], att[:, :], ident).then_inc(pe_aT, 1)

            def out_proj(i, c):
                seq_done(pe, a_aT, i, c)
                pe.matmul(Mi[:, 0:D], aT[:, :], wsm[:, WO:WO + D], start=True, stop=True).then_inc(pe_wo, 1)

            def n_T(i, c):
                seq_done(pe, v_n, i, c)
                pe.transpose(Qb[:, 0:T], nr[:, c % 2, :], ident).then_inc(pe_nT, 1)

            pe.wait_ge(v_setup, 2 + 2 * COPIES + 6)
            x_T(0, 0)
            qkv(0, 0)
            pe.wait_ge(p_set, 4)
            scores(0, 0)

            def pair(i):
                for w in range(8):
                    c, s = divmod(w, SETS)
                    if has(i, (w + 1) // SETS):
                        scores(i, w + 1)
                    if not isinstance(i, int) or 4 * i + w >= 2:
                        values(i, w - 2)
                    if s == 0 and has(i, c + 1):
                        x_T(i, c + 1)
                    if s == 1 and has(i, c + 1):
                        qkv(i, c + 1)
                    if s == 3 and has(i, c - 2):
                        seq_done(pe, v_q, i, c + 1 if has(i, c + 1) else c)
                        n_T(i, c - 2)
                    scores_T(i, w)
                    if s == 2 and has(i, c - 1):
                        seq_done(pe, a_v, i, c + 1 if has(i, c + 1) else c)
                        att_T(i, c - 1)
                    if s == 3 and has(i, c - 1):
                        out_proj(i, c - 1)
            over_pairs(pe, pair)
            last = B - 2
            values(last, 6)
            values(last, 7)
            seq_done(pe, v_x2, last, 0)
            att_T(last, 1)
            n_T(last, 0)
            out_proj(last, 1)
            seq_done(pe, a_nT, last, 0)
            n_T(last, 1)

            for b in range(B):
                pe.wait_ge(a_nT, b + 1)
                mm = pe.matmul(bank[0][:, b * E:(b + 1) * E], NT[:, b * T:(b + 1) * T], wsm[:, WR:WR + E], start=(b == 0),
                               stop=(b == B - 1))
            mm.then_inc(pe_lg, 1)
            for h in range(2):
                hs = slice(h * HALF, (h + 1) * HALF)
                for o, bk in ((WSG, bank[3 + h]), (WSU, bank[5 + h])):
                    pe.matmul(bk[:, :], wsm[:, o:o + SF], NT[:, hs], start=True, stop=True).then_inc(pe_sgu, 1)

            pe.wait_ge(v_rt, V_MB)
            mb = Mb[:, :, :].rearrange("p b e -> p (b e)")
            pe.matmul(bank[1][:, 0:(B + 1) * E], ltb[:, :], mb, start=True, stop=False)
            for s in range(1, B + 1):
                last = pe.matmul(bank[1][:, s * E:(B + 1) * E], onesb[:, :], mb[:, 0:(B + 1 - s) * E], start=False, stop=(s == B))
            last.then_inc(pe_rank, 1)
            pe.wait_ge(v_rt, V_BV)
            for n in range(2 * B):
                last = pe.matmul(bank[2][:, 0:2 * TT], Aoh[:, n, :], Bv[:, n].rearrange("p n i -> p (n i)"), start=(n == 0),
                                 stop=(n == 2 * B - 1))
            last.then_inc(pe_tab, 1)
            for h in range(2):
                pe.wait_ge(v_sh, h + 1)
                for b in range(B // 2):
                    t = h * HALF + b * T
                    last = pe.matmul(bank[h][:, b * D:(b + 1) * D], sH[:, t:t + T], wsm[:, WSD:WSD + D], start=True, stop=True)
                last.then_inc(pe_sy, 1)

            def tok_T(n, m):
                done(pe, gat, n, m, 16)
                done(pe, v_gl, n, m - 1)
                pe.transpose(bank[4][:, 0:T], XG[:, m % 4, :], ident).then_inc(pe_gT[m % 4], 1)

            pe.wait_ge(v_x3, 2)
            pe.wait_ge(ld_d, 16)
            for c in range(2):
                pe.wait_ge(v_wl, E // 2)
            tok_T(0, 0)

            def step(n, m):
                k = 4 * n + m
                if tile_in(n, m):
                    e = pe.value_load(goff[0:1, bass.ds(k, 1)], min_val=0, max_val=(E - 1) * GU)
                    done(pe, a_gh, n, m)
                    done(pe, v_gl, n, m)
                    done(pe, a_s, n, m - 2)
                    done(pe, v_h, n, m - 2)
                    gh, gl = gTh[:, m % 2, :], gTl[:, m % 2, :]
                    for o, bk in ((0, bank[m % 2]), (F, bank[2 + m % 2])):
                        w = bass.ds(e + o, F)
                        pe.matmul(bk[:, 0:F], gh, WH[:, w], start=True, stop=False)
                        pe.matmul(bk[:, 0:F], gl, WH[:, w], start=False, stop=False)
                        last = pe.matmul(bk[:, 0:F], gh, WL[:, w], start=False, stop=True)
                    last.then_inc(pe_gu[m % 4], 1)
                if tile_in(n, m - 1):
                    done(pe, v_h, n, m - 1)
                    done(pe, a_hT, n, m - 3)
                    for f in range(FC):
                        last = pe.transpose(bank[5 + (m - 1) % 2][:, f * T:(f + 1) * T], gH[:, (m - 1) % 2, f * T:(f + 1) * T], ident)
                    last.then_inc(pe_hT[(m - 1) % 4], 1)
                if tile_in(n, m + 1):
                    tok_T(n, m + 1)
                if tile_in(n, m - 2):
                    e = pe.value_load(doff[0:1, bass.ds(k - 2, 1)], min_val=0, max_val=(E - 1) * DN)
                    done(pe, a_hT, n, m - 2)
                    done(pe, a_y, n, m - 3)
                    for f in range(FC):
                        last = pe.matmul(bank[7][:, 0:D], hT[:, m % 2, f * T:(f + 1) * T], WD[:, bass.ds(e + f * D, D)],
                                         start=(f == 0), stop=(f == FC - 1))
                    last.then_inc(pe_y[(m - 2) % 4], 1)
            over_tiles(pe, step)


V_MB = 5 + 5 + 6 + 1
V_DP = V_MB + 1
V_BV = V_DP + 6 + 3 + 4 + 2 + 2


def kernel(**inputs):
    import numpy as _np
    import concourse.bacc as _bacc
    from concourse import mybir as _mybir
    from concourse.bass_utils import run_bass_kernel_spmd as _run

    a = {k: _np.asarray(v) for k, v in inputs.items()}
    p = _np.arange(T)
    const = _np.zeros((T, CONST), _np.float32)
    const[:, C_ID:C_ID + T] = p[:, None] == p[None, :]
    const[:, C_LT:C_LT + T] = p[:, None] < p[None, :]
    const[:, C_CM:C_CM + T] = _np.where(p[:, None] >= p[None, :], 0.0, -1e30)
    const[:, C_SL:C_SL + T] = p
    const[:, C_TL:C_TL + TT] = _np.arange(TT)
    const[:, C_LQ] = (p % 32) // HD == 1
    const[:, C_LK] = (p % 32) // HD == 2
    const[:, C_EW:C_EW + E] = E - _np.arange(E)
    const[:, C_J:C_J + E] = T * _np.arange(E)
    kk = _np.repeat(_np.arange(2), B)
    const[:, C_PK:C_PK + 2 * B] = 2 * p[:, None] + kk[None, :] + 1
    const[:, C_TK:C_TK + 2 * B] = 2 * T * _np.tile(_np.arange(B), 2)
    const[:, C_ON:C_ON + 2] = 1.0
    wsmall = _np.concatenate([a[n].T for n in ("L0_xattn_Wq", "L0_xattn_Wk", "L0_xattn_Wv", "L0_xattn_Wo",
                                               "L0_ffn_shared_gate_up_w", "L0_ffn_shared_down_w", "L0_ffn_router_w")], axis=1)
    gu = a["L0_ffn_gate_up_w"].transpose(0, 2, 1)
    dn = a["L0_ffn_down_w"].transpose(0, 2, 1).reshape(E, FC, T, D).transpose(0, 2, 1, 3).transpose(1, 0, 2, 3).reshape(T, E * FC * D)
    arrays = {
        "x": a["x"].reshape(B * T, D),
        "ctxT": a["ctx_1024"].reshape(B * T, D).T,
        "vec": _np.concatenate([a["L0_ffn_ln_gamma"], a["L0_ffn_ln_beta"], a["g_xattn"], a["g_ffn"]])[None, :],
        "wsmall": wsmall,
        "wgu": gu.reshape(E * D, GU),
        "wdn": dn,
        "const": const,
    }
    nc = _bacc.Bacc("TRN2", target_bir_lowering=False, num_devices=1)
    ins, args = {}, []
    for name, v in arrays.items():
        ins["in_" + name] = _np.ascontiguousarray(v)
        args.append(nc.dram_tensor("in_" + name, v.shape, _mybir.dt.from_np(v.dtype), kind="ExternalInput").ap())
    args.append(nc.dram_tensor("out", (B * T, D), _mybir.dt.float32, kind="ExternalOutput").ap())
    gated_layer(nc, *args)
    r = _run(nc, [ins], core_ids=[0])
    return r.results[0]["out"].reshape(B, T, D)
```

```python
import concourse.bass as bass
from concourse import mybir
from contextlib import ExitStack

B, T, D = 8, 128, 128
H, HD = 16, 8
SETS, ROWS = 4, 4
COPIES = 3
E, F = 8, 384
FC = F // T
SF = 128
PAIRS = 2 * B * T
TILES = PAIRS // T + E - 1
TT = TILES + 1
HALF = B * T // 2
UNITS = SETS * B
EPS = 1e-5
GU, DN = 2 * F, FC * D
WARM_SETS = (1,)
CREDIT = 16
SKIP = 4096.0

WQ, WK, WV, WO, WSG, WSU, WSD, WR = 0, 128, 256, 384, 512, 640, 768, 896
WSMALL = WR + E
C_ID, C_LT, C_CM, C_SL, C_TL = 0, 128, 256, 384, 512
C_LQ, C_LK, C_EW, C_J, C_PK, C_TK, C_ON = 536, 537, 538, 546, 554, 570, 586
CONST = 588


def gated_layer(nc, x_h, ctxT_h, vec_h, wsmall_h, wgu_h, wdn_h, const_h, out_h):
    f32, f32r, bf16, i32 = mybir.dt.float32, mybir.dt.float32r, mybir.dt.bfloat16, mybir.dt.int32
    ALU, ACT, AX = mybir.AluOpType, mybir.ActivationFunctionType, mybir.AxisListType.X
    ctx = ExitStack()
    with ctx:
        def sb(name, shape, dt=f32):
            return ctx.enter_context(nc.sbuf_tensor(name, shape, dt))

        def sem(name):
            return ctx.enter_context(nc.semaphore(name))

        norm_d = nc.dram_tensor("norm_d", (B * T, D), f32, kind="Internal").ap()
        y_d = nc.dram_tensor("y_d", (PAIRS, D), f32, kind="Internal").ap()

        X = sb("X", [T, B * D])
        cT = sb("cT", [D, 2, T])
        vec = sb("vec", [T, 2 * D + 2])
        wsm = sb("wsm", [D, WSMALL])
        wstk = sb("wstk", [D, 2, SETS, 4 * 32])
        cst = sb("cst", [T, CONST])
        identb = sb("identb", [T, T], bf16)
        ltb = sb("ltb", [T, T], bf16)
        maskb = sb("maskb", [T, SETS, T], bf16)
        onesb = sb("onesb", [T, T], bf16)
        slotb = sb("slotb", [T, T], bf16)
        tg = sb("tg", [T, 2])
        st1 = sb("st1", [T, B, 6])
        mv1 = sb("mv1", [T, B, 2])
        ve1 = sb("ve1", [T, B])
        r1 = sb("r1", [T, B])
        mhalf = sb("mhalf", [T, B])
        xn = sb("xn", [T, 2, D])
        xT = sb("xT", [D, T])
        tq = sb("tq", [T, SETS, T], f32r)
        tk = sb("tk", [T, SETS, T], f32r)
        qS = sb("qS", [T, 2, SETS, T], f32r)
        kS = sb("kS", [T, 2, SETS, ROWS, T], f32r)
        kC = sb("kC", [T, SETS, T], f32r)
        V = sb("V", [T, 2, H, HD + 1])
        nm = sb("nm", [T, 4, SETS])
        P = sb("P", [T, 2, ROWS, T])
        PT = sb("PT", [T, 2, ROWS, T])
        rec = sb("rec", [T, H])
        att = sb("att", [T, D])
        aT = sb("aT", [D, T])
        X2 = sb("X2", [T, B * D])
        x2 = sb("x2", [T, 2, D])
        st2 = sb("st2", [T, 2, 6])
        mv2 = sb("mv2", [T, 2, 2])
        ve2 = sb("ve2", [T, 2])
        r2 = sb("r2", [T, 2])
        ng = sb("ng", [T, D])
        nr = sb("nr", [T, 2, D])
        NT = sb("NT", [D, B * T])
        wst = sb("wst", [D, 2, GU])
        WH = sb("WH", [D, E * GU], f32r)
        WL = sb("WL", [D, E * GU], f32r)
        WD = sb("WD", [D, E * GU])
        lg = sb("lg", [T, B, E])
        col = {n: sb("c_" + n, [T, B]) for n in ("mx", "sum", "rs", "p1", "w1", "p2", "w2", "dp", "e2", "o2", "g1", "g2")}
        ex = sb("ex", [T, B, E])
        pr = sb("pr", [T, B, E])
        eq = sb("eq", [T, 2, B, E])
        ew = sb("ew", [T, 2, B, E])
        M = sb("M", [T, 2, B, E])
        pr2 = sb("pr2", [T, B, E])
        Mb = sb("Mb", [T, B + 1, E], bf16)
        over = sb("over", [T, E, E])
        nt = sb("nt", [T, E])
        inc = sb("inc", [T, E])
        ts = sb("ts", [T, E])
        base = sb("base", [T, E])
        dest = sb("dest", [T, B, E])
        md = sb("md", [T, 2, B, E])
        slot = sb("slot", [T, 2, B])
        sloti = sb("sloti", [T, 2, B], i32)
        inti = sb("inti", [T, 2, 2, B], i32)
        intb = sb("intb", [T, 2 * B], bf16)
        Aoh = sb("Aoh", [T, 2 * B, T], bf16)
        tiles_of = sb("tiles_of", [T, 2 * B, TT])
        Bv = sb("Bv", [T, 2 * B, 2, TT], bf16)
        id1 = sb("id1", [T, TT])
        none = sb("none", [T, TT])
        gi = sb("gi", [T, TT])
        si = sb("si", [T, TT])
        gidx = sb("gidx", [T, TT], i32)
        gtok = sb("gtok", [T, TT], i32)
        sidx = sb("sidx", [T, TT], i32)
        gring = sb("gring", [T, 4], i32)
        sring = sb("sring", [T, 2], i32)
        cmpe = sb("cmpe", [1, TT, E])
        eidf = sb("eidf", [1, TT])
        goff = sb("goff", [1, TT], i32)
        sS = sb("sS", [SF, B * T])
        sU = sb("sU", [SF, B * T])
        sH = sb("sH", [SF, B * T])
        sY = sb("sY", [T, B * D])
        XG = sb("XG", [T, 4, D])
        gTh = sb("gTh", [D, 2, T], f32r)
        gTl = sb("gTl", [D, 2, T], f32r)
        gS = sb("gS", [T, 2, F])
        gH = sb("gH", [T, 2, F])
        hT = sb("hT", [T, 2, F])
        Y = sb("Y", [T, 2, D])
        YG = sb("YG", [T, B, 2, D])
        out_sb = sb("out_sb", [T, B, D])

        bank = [ctx.enter_context(nc.psum_tensor(f"bank{n}", [128, 512], f32)) for n in range(8)]
        Sb, Ob, Tb, Qb, Mi = bank[0:4], bank[4], bank[5], bank[6], bank[7]
        LG, RK, TAB = bank[0], bank[4], bank[6]
        SG, SU, SY = (bank[1], bank[3]), (bank[2], bank[5]), (bank[7], bank[1])

        def sems(name, n):
            return [sem(f"{name}{m}") for m in range(n)]

        ld_small, ld_const, ld_vec, ld_d = (sem("ld_" + n) for n in ("small", "const", "vec", "d"))
        ld_x, ld_c, ld_w, st_k, st_n = (sems(n, 2) for n in ("ld_x", "ld_c", "ld_w", "st_k", "st_n"))
        ld_y = sems("ld_y", B // 2)
        pe_S, pe_T, pe_PV, v_max, a_exp, a_PT = (sems(n, SETS) for n in ("pe_S", "pe_T", "pe_PV", "v_max", "a_exp", "a_PT"))
        pe_xT, pe_q, pe_k, pe_v, pe_aT, pe_wo, pe_nT = (sem("pe_" + n) for n in ("xT", "q", "k", "v", "aT", "wo", "nT"))
        v_xn, v_q, v_kc, v_k, v_rec, v_att, v_x2, v_st2, v_mv2, v_ve2, v_ng, v_n = (
            sem("v_" + n) for n in ("xn", "q", "kc", "k", "rec", "att", "x2", "st2", "mv2", "ve2", "ng", "n"))
        a_xT, a_tq, a_tk, a_v, a_aT, a_nT, a_wh = (
            sem("a_" + n) for n in ("xT", "tq", "tk", "v", "aT", "nT", "wh"))
        p_r2, p_x2, p_wl = (sem("p_" + n) for n in ("r2", "x2", "wl"))
        v_setup, v_st1, v_ve1, p_set, p_r1, a_tg = (sem(n) for n in ("v_setup", "v_st1", "v_ve1", "p_set", "p_r1", "a_tg"))
        pe_lg, pe_rank, pe_tab, v_rt, a_ex, a_e2, v_ready = (
            sem(n) for n in ("pe_lg", "pe_rank", "pe_tab", "v_rt", "a_ex", "a_e2", "v_ready"))
        pe_sgu, pe_sy, a_ss, a_sy, p_sh, p_x3 = (sem(n) for n in ("pe_sgu", "pe_sy", "a_ss", "a_sy", "p_sh", "p_x3"))
        gat, sca, pe_gT, pe_gu, pe_hT, pe_y, a_gh, v_gl, a_s, v_h, a_hT, a_y, v_gi, v_si = (
            sems(n, 4) for n in ("gat", "sca", "pe_gT", "pe_gu", "pe_hT", "pe_y", "a_gh", "v_gl", "a_s", "v_h", "a_hT", "a_y",
                                 "v_gi", "v_si"))
        p_go, v_go, p_bv = sem("p_go"), sem("v_go"), sem("p_bv")
        v_f1, v_out, st_o = sem("v_f1"), sem("v_out"), sem("st_o")

        block = ctx.enter_context(nc.Block())

        def done(eng, list_, n, m, by=1):
            q, m = divmod(m, 4)
            if not isinstance(n, int) or n + q >= 0:
                eng.wait_ge(list_[m], (n + (q + 1)) * by)

        def unit_done(eng, list_, i, w):
            q, m = divmod(w, SETS)
            if not isinstance(i, int) or i + q >= 0:
                eng.wait_ge(list_[m], i + (q + 1))

        def seq_done(eng, s, i, c):
            if not isinstance(i, int) or i + c >= 0:
                eng.wait_ge(s, i + (c + 1))

        def load_done(eng, list_, i, c, by=1):
            q, m = divmod(c, 2)
            eng.wait_ge(list_[m], i * (8 * by) + 16 * by * (q + 1))

        def has(i, c):
            return not isinstance(i, int) or 0 <= i + c < B

        def seq(b):
            return bass.ds(b * T, T)

        def over_pairs(eng, body):
            body(0)
            with eng.Fori(2, B - 3, 2) as i:
                body(i)
            body(B - 2)

        def over_tiles(eng, step):
            last = (TILES - 4) // 4
            for m in range(4):
                step(0, m)
            with eng.Fori(1, last) as n:
                for m in range(4):
                    step(n, m)
            for k in range(4 * last, TILES + 2):
                step(k // 4, k % 4)

        def tile_in(n, m):
            return not isinstance(n, int) or 0 <= 4 * n + m < TILES

        def load_y(eng, parts):
            for m in range(4):
                eng.wait_ge(sca[m], 16 * len(range(m, TILES, 4)))
            yv = y_d.rearrange("(b p k) d -> p b (k d)", b=B, k=2)
            for h in parts:
                bs = slice(2 * h, 2 * h + 2)
                eng.dma_start(YG[:, bs, :, :].rearrange("p b k d -> p b (k d)"), yv[:, bs, :]).then_inc(ld_y[h], 16)

        @block.sync
        def _(sp):
            def load_x(h):
                bs = slice(h * B // 2, (h + 1) * B // 2)
                sp.dma_start(X[:, :].rearrange("p (b d) -> p b d", b=B)[:, bs, :],
                             x_h.rearrange("(b p) d -> p b d", b=B)[:, bs, :]).then_inc(ld_x[h], 16)

            def load_c(b, c):
                sp.dma_start(cT[:, c, :], ctxT_h[:, seq(b)]).then_inc(ld_c[c], 16)

            def load_w(e, c):
                sp.dma_start(wst[:, c, :], wgu_h[bass.ds(e * D, D), :]).then_inc(ld_w[c], 16)

            for c in range(2):
                sp.sem_inc(st_n[c], CREDIT)
            sp.dma_start(wsm[:, :], wsmall_h).then_inc(ld_small, 16)
            load_c(0, 0)
            load_x(0)
            load_x(1)
            load_c(1, 1)
            sp.dma_start(vec[:, :], vec_h.to_broadcast((T, 2 * D + 2))).then_inc(ld_vec, 16)
            load_w(0, 0)
            load_w(1, 1)
            sp.dma_start(WD[:, :].rearrange("p (e w) -> p e w", e=E)[:, :, 0:DN],
                         wdn_h.rearrange("p (e w) -> p e w", e=E)).then_inc(ld_d, 16)

            def stack(i, c):
                seq_done(sp, v_kc, i, c)
                for j in (2, 3):
                    r = slice(32 * j, 32 * j + 32)
                    sp.dma_start(kS[r, c % 2, :, j, :].bitcast(f32), kC[r, :, :].bitcast(f32)).then_inc(st_k[c % 2], 16)

            stack(0, 0)

            def pair(i):
                for c in range(2):
                    b = i + c
                    if has(i, c + 2):
                        seq_done(sp, pe_v, i, c)
                        load_c(b + 2, c)
                    if has(i, c + 1):
                        stack(i, c + 1)
                    if has(i, c - 2):
                        seq_done(sp, v_n, i, c - 2)
                        sp.dma_start(norm_d[seq(b - 2), :], nr[:, c, :]).then_inc(st_n[c], 16)
                    if has(i, c + 2):
                        seq_done(sp, a_wh, i, c)
                        seq_done(sp, p_wl, i, c)
                        load_w(b + 2, c)
            over_pairs(sp, pair)
            for c in range(2):
                seq_done(sp, v_n, B - 2, c)
                sp.dma_start(norm_d[seq(B - 2 + c), :], nr[:, c, :]).then_inc(st_n[c], 16)
            load_y(sp, (0, 1))
            for h in range(B // 2):
                bs = slice(2 * h, 2 * h + 2)
                sp.wait_ge(v_out, 2 * h + 2)
                sp.dma_start(out_h.rearrange("(b p) d -> p b d", b=B)[:, bs, :], out_sb[:, bs, :]).then_inc(st_o, 16)
            sp.wait_ge(st_o, 16 * B // 2)

        @block.gpsimd
        def _(pool):
            pool.memset(mhalf[:, :], -0.5).then_inc(p_set, 1)
            for c in range(2):
                pool.memset(kS[:, c].bitcast(f32), 0.0).then_inc(p_set, 1)
            pool.memset(V[:, :, :, HD:HD + 1], 1.0).then_inc(p_set, 1)
            pool.memset(Mb[:, B, :], 0.0).then_inc(p_set, 1)
            pool.wait_ge(p_set, 1)
            pool.wait_ge(v_ve1, 1)
            pool.tensor_tensor(r1[:, :], ve1[:, :], mhalf[:, :], ALU.pow).then_inc(p_r1, 1)

            def rstd2(i, c):
                seq_done(pool, v_ve2, i, c)
                pool.tensor_tensor(r2[:, c % 2:c % 2 + 1], ve2[:, c % 2:c % 2 + 1], mhalf[:, 0:1], ALU.pow).then_inc(p_r2, 1)

            def keep(i, c):
                seq_done(pool, v_x2, i, c)
                pool.sem_inc(p_go, 1)
                pool.tensor_copy(X2[:, seq(i + c)], x2[:, c % 2, :]).then_inc(p_x2, 1)

            def w_lo(i, c):
                e = bass.ds((i + c) * GU, GU)
                seq_done(pool, a_wh, i, c)
                pool.sem_inc(p_go, 1)
                pool.tensor_tensor(WL[:, e], wst[:, c, :], WH[:, e].bitcast(f32), ALU.subtract).then_inc(p_wl, 1)

            def pair(i):
                for c in range(2):
                    if has(i, c - 2):
                        rstd2(i, c - 2)
                    if has(i, c - 2):
                        keep(i, c - 2)
                    w_lo(i, c)
            over_pairs(pool, pair)
            for c in range(2):
                rstd2(B - 2, c)
                keep(B - 2, c)

            for h in range(2):
                hs = slice(h * HALF, (h + 1) * HALF)
                pool.wait_ge(a_ss, 2 * h + 2)
                pool.tensor_tensor(sH[:, hs], sS[:, hs], sU[:, hs], ALU.mult).then_inc(p_sh, 1)

            pool.wait_ge(v_rt, V_TI)
            for n, o in ((0, C_PK), (1, C_TK)):
                pool.tensor_tensor(Bv[:, :, n, :], tiles_of[:, :, :],
                                   cst[:, o:o + 2 * B].unsqueeze(2).to_broadcast((T, 2 * B, TT)), ALU.mult).then_inc(p_bv, 1)

            pool.wait_ge(v_ready, 1)
            for c in range(2):
                pool.wait_ge(st_n[c], CREDIT + 16 * B // 2)

            def gather(n, m):
                done(pool, v_gi, n, m)
                done(pool, pe_gT, n, m - 4)
                pool.sem_inc(p_go, 1)
                pool.indirect_dma_start(XG[:, m % 4, :], None, norm_d, bass.IndirectOffsetOnAxis(gring[:, m % 4:m % 4 + 1], 0),
                                        bounds_check=B * T - 1, oob_is_err=False).then_inc(gat[m % 4], 16)

            def scatter(n, m):
                done(pool, v_si, n, m)
                done(pool, a_y, n, m)
                pool.sem_inc(p_go, 1)
                pool.indirect_dma_start(y_d, bass.IndirectOffsetOnAxis(sring[:, m % 2:m % 2 + 1], 0), Y[:, m % 2, :], None,
                                        bounds_check=PAIRS - 1, oob_is_err=False).then_inc(sca[m % 4], 16)
            for m in range(4):
                gather(0, m)
            pool.wait_ge(p_x2, B)
            for h in range(2):
                hs = slice(h * HALF, (h + 1) * HALF)
                pool.wait_ge(a_sy, h + 1)
                pool.tensor_tensor(X2[:, hs], X2[:, hs], sY[:, hs], ALU.add).then_inc(p_x3, 1)

            def step(n, m):
                if tile_in(n, m + 4):
                    gather(n, m + 4)
                if tile_in(n, m - 2):
                    scatter(n, m - 2)
            over_tiles(pool, step)

        @block.scalar
        def _(act):
            act.dma_start(cst[:, :], const_h).then_inc(ld_const, 16)
            act.wait_ge(ld_vec, 16)
            act.activation(tg[:, :], vec[:, 2 * D:2 * D + 2], ACT.Tanh).then_inc(a_tg, 1)
            act.wait_ge(ld_const, 16)

            def x_out(i, c):
                seq_done(act, pe_xT, i, c)
                seq_done(act, pe_q, i, c - 1)
                act.activation(xT[:, :], Qb[:, 0:T], ACT.Copy).then_inc(a_xT, 1)

            def k_low(i, c):
                seq_done(act, pe_k, i, c)
                seq_done(act, v_kc, i, c - 1)
                act.activation(tk[:, :, :], Qb[:, :].rearrange("p (s t) -> p s t", s=SETS), ACT.Copy,
                               scale=cst[:, C_LK:C_LK + 1]).then_inc(a_tk, 1)

            def q_low(i, c):
                seq_done(act, pe_q, i, c)
                seq_done(act, v_q, i, c - 1)
                act.activation(tq[:, :, :], Qb[:, :].rearrange("p (s t) -> p s t", s=SETS), ACT.Copy,
                               scale=cst[:, C_LQ:C_LQ + 1]).then_inc(a_tq, 1)

            def v_out(i, c):
                seq_done(act, pe_v, i, c)
                unit_done(act, pe_PV, i, SETS * (c - 1) - 1)
                act.activation(V[:, c % 2, :, 0:HD], Mi[:, 0:D].rearrange("p (h e) -> p h e", h=H), ACT.Copy)\
                   .then_inc(a_v, 1)

            def expo(i, w):
                unit_done(act, v_max, i, w)
                unit_done(act, pe_T, i, w - 2)
                for j in range(ROWS):
                    last = act.activation(P[:, w % 2, j, :], Sb[w % 4][:, j * T:(j + 1) * T], ACT.Exp,
                                          bias=nm[:, w % 4, j:j + 1])
                last.then_inc(a_exp[w % 4], 1)

            def p_out(i, w):
                unit_done(act, pe_T, i, w)
                unit_done(act, pe_PV, i, w - 2)
                act.activation(PT[:, w % 2], Tb[:, :].rearrange("p (j t) -> p j t", j=ROWS), ACT.Copy)\
                   .then_inc(a_PT[w % 4], 1)

            def att_out(i, c):
                seq_done(act, pe_aT, i, c)
                seq_done(act, pe_wo, i, c - 1)
                act.activation(aT[:, :], Mi[:, 0:T], ACT.Copy).then_inc(a_aT, 1)

            def n_out(i, c):
                seq_done(act, pe_nT, i, c)
                act.activation(NT[:, seq(i + c)], Qb[:, 0:T], ACT.Copy).then_inc(a_nT, 1)

            def w_hi(i, c):
                load_done(act, ld_w, i, c)
                act.activation(WH[:, bass.ds((i + c) * GU, GU)], wst[:, c, :], ACT.Copy).then_inc(a_wh, 1)

            k_low(0, 0)
            x_out(0, 0)
            q_low(0, 0)
            v_out(0, 0)
            x_out(0, 1)

            def pair(i):
                for w in range(8):
                    c, s = divmod(w, SETS)
                    if s == 0 and has(i, c + 1):
                        k_low(i, c + 1)
                    if s == 1 and has(i, c + 1):
                        q_low(i, c + 1)
                    if s == 2 and has(i, c + 2):
                        x_out(i, c + 2)
                    if s == 3 and has(i, c - 1):
                        att_out(i, c - 1)
                    if s == 3 and has(i, c - 2):
                        n_out(i, c - 2)
                    expo(i, w)
                    if not isinstance(i, int) or 4 * i + w >= 1:
                        p_out(i, w - 1)
                    if s == 0:
                        w_hi(i, c)
                    if s == 2 and has(i, c + 1):
                        v_out(i, c + 1)
            over_pairs(act, pair)
            last = B - 2
            p_out(last, 7)
            att_out(last, 1)
            n_out(last, 0)
            n_out(last, 1)

            act.wait_ge(v_rt, 2)
            act.activation(ex[:, :, :], lg[:, :, :], ACT.Exp).then_inc(a_ex, 1)
            act.wait_ge(v_rt, V_DP)
            act.activation(col["e2"][:, :], col["dp"][:, :], ACT.Exp).then_inc(a_e2, 1)

            for h in range(2):
                hs = slice(h * HALF, (h + 1) * HALF)
                act.wait_ge(pe_sgu, 2 * h + 2)
                act.activation(sS[:, hs], SG[h][:, :], ACT.Silu).then_inc(a_ss, 1)
                act.activation(sU[:, hs], SU[h][:, :], ACT.Copy).then_inc(a_ss, 1)
            for h in range(2):
                act.wait_ge(pe_sy, h + 1)
                act.activation(sY[:, h * HALF:(h + 1) * HALF], SY[h][:, :], ACT.Copy, scale=tg[:, 1:2]).then_inc(a_sy, 1)

            def tok_hi(n, m):
                done(act, pe_gT, n, m)
                done(act, pe_gu, n, m - 2)
                act.activation(gTh[:, m % 2, :], bank[4][:, 0:T], ACT.Copy).then_inc(a_gh[m % 4], 1)

            tok_hi(0, 0)

            def step(n, m):
                if tile_in(n, m + 1):
                    tok_hi(n, m + 1)
                if tile_in(n, m):
                    done(act, pe_gu, n, m)
                    done(act, v_h, n, m - 2)
                    act.activation(gS[:, m % 2, :], bank[m % 2][:, 0:F], ACT.Silu).then_inc(a_s[m % 4], 1)
                if tile_in(n, m - 2):
                    done(act, pe_y, n, m - 2)
                    done(act, sca, n, m - 4, 16)
                    act.activation(Y[:, m % 2, :], bank[7][:, 0:D], ACT.Copy).then_inc(a_y[(m - 2) % 4], 1)
                if tile_in(n, m - 1):
                    done(act, pe_hT, n, m - 1)
                    act.activation(hT[:, (m - 1) % 2, :], bank[5 + (m - 1) % 2][:, 0:F], ACT.Copy).then_inc(a_hT[(m - 1) % 4], 1)
            over_tiles(act, step)
            load_y(act, (2, 3))

        @block.vector
        def _(dve):
            for n in range(2):
                dve.memset(wstk[:, n], 0.0).then_inc(v_setup, 1)
            dve.wait_ge(ld_small, 16)
            dve.wait_ge(v_setup, 2)
            for n, o in ((0, WQ), (1, WK)):
                for r in range(COPIES):
                    d = wstk[:, n].rearrange("p s (j r e) -> p (s j) r e", j=ROWS, e=HD)
                    dve.tensor_scalar(d[:, :, r, :], wsm[:, o:o + D].rearrange("p (h e) -> p h e", e=HD),
                                      HD ** -0.5 if n == 0 else 1.0, None, ALU.mult).then_inc(v_setup, 1)
            for h in range(2):
                dve.wait_ge(ld_x[h], 16)
                for b in range(h * B // 2, (h + 1) * B // 2):
                    dve.bn_stats(st1[:, b, :], X[:, b * D:(b + 1) * D]).then_inc(v_st1, 1)
            for b in range(B):
                dve.wait_ge(v_st1, b + 1)
                dve.bn_aggr(mv1[:, b, :], st1[:, b, :]).then_inc(v_st1, 1)
            dve.wait_ge(v_st1, 2 * B)
            dve.tensor_scalar(ve1[:, :], mv1[:, :, 1], EPS, None, ALU.add).then_inc(v_ve1, 1)
            dve.wait_ge(ld_const, 16)
            for dst, src in ((identb[:, :], C_ID), (ltb[:, :], C_LT), (slotb[:, :], C_SL)):
                dve.tensor_copy(dst, cst[:, src:src + T]).then_inc(v_setup, 1)
            dve.tensor_copy(maskb[:, :, :], cst[:, C_CM:C_CM + T].unsqueeze(1).to_broadcast((T, SETS, T))).then_inc(v_setup, 1)
            dve.tensor_copy(onesb[:, :], cst[:, C_ON:C_ON + 1].to_broadcast((T, T))).then_inc(v_setup, 1)

            def normalise(i, c):
                seq_done(dve, pe_xT, i, c - 2)
                b = i + c
                dve.tensor_scalar(xn[:, c % 2, :], X[:, seq(b)], mv1[:, bass.ds(b, 1), 0], r1[:, bass.ds(b, 1)],
                                  ALU.subtract, ALU.mult).then_inc(v_xn, 1)

            def stack_k(i, c):
                seq_done(dve, a_tk, i, c)
                if has(i, c - 1):
                    load_done(dve, st_k, i, c - 1, 2)
                unit_done(dve, pe_S, i, SETS * (c - 1) - 1)
                dve.tensor_tensor(kC[:, :, :], Qb[:, :].rearrange("p (s t) -> p s t", s=SETS), tk[:, :, :].bitcast(f32),
                                  ALU.subtract).then_inc(v_kc, 1)
                seq_done(dve, v_kc, i, c)
                for j in (0, 1):
                    r = slice(32 * j, 32 * j + 32)
                    last = dve.tensor_copy(kS[r, c % 2, :, j, :], kC[r, :, :])
                last.then_inc(v_k, 1)

            def stack_q(i, c):
                seq_done(dve, a_tq, i, c)
                dve.tensor_tensor(qS[:, c % 2], Qb[:, :].rearrange("p (s t) -> p s t", s=SETS), tq[:, :, :].bitcast(f32),
                                  ALU.subtract).then_inc(v_q, 1)

            def negmax(i, w):
                unit_done(dve, pe_S, i, w)
                unit_done(dve, a_exp, i, w - 4)
                dve.tensor_reduce(nm[:, w % 4, :], Sb[w % 4][:, :].rearrange("p (j t) -> p j t", j=ROWS), AX, ALU.max,
                                  negate=True).then_inc(v_max[w % 4], 1)

            def weigh(i, c):
                o = Ob[:, 0:H * (HD + 1)].rearrange("p (h e) -> p h e", h=H)
                unit_done(dve, pe_PV, i, SETS * c + SETS - 1)
                dve.reciprocal(rec[:, :], o[:, :, HD]).then_inc(v_rec, 1)
                seq_done(dve, v_rec, i, c)
                seq_done(dve, pe_aT, i, c - 1)
                dve.tensor_tensor(att[:, :].rearrange("p (h e) -> p h e", h=H), o[:, :, 0:HD],
                                  rec[:, :].unsqueeze(2).to_broadcast((T, H, HD)), ALU.mult).then_inc(v_att, 1)

            def residual(i, c):
                b = i + c
                seq_done(dve, pe_wo, i, c)
                dve.scalar_tensor_tensor(x2[:, c % 2, :], Mi[:, 0:D], tg[:, 0:1], X[:, seq(b)], ALU.mult,
                                         ALU.add).then_inc(v_x2, 1)
                seq_done(dve, v_x2, i, c)
                dve.bn_stats(st2[:, c % 2, :], x2[:, c % 2, :]).then_inc(v_st2, 1)
                seq_done(dve, v_st2, i, c)
                dve.sem_inc(v_go, 1)
                dve.bn_aggr(mv2[:, c % 2, :], st2[:, c % 2, :]).then_inc(v_mv2, 1)
                seq_done(dve, v_mv2, i, c)
                dve.tensor_scalar(ve2[:, c % 2:c % 2 + 1], mv2[:, c % 2, 1:2], 1.0 + EPS, EPS * EPS, ALU.mult,
                                  ALU.add).then_inc(v_ve2, 1)

            def normed(i, c):
                q, m = divmod(c, 2)
                dve.wait_ge(st_n[m], i * 8 + 16 * (q + 1))
                dve.scalar_tensor_tensor(ng[:, :], x2[:, c % 2, :], mv2[:, c % 2, 0:1], vec[:, 0:D], ALU.subtract,
                                         ALU.mult).then_inc(v_ng, 1)
                seq_done(dve, v_ng, i, c)
                seq_done(dve, p_r2, i, c)
                dve.scalar_tensor_tensor(nr[:, c % 2, :], ng[:, :], r2[:, c % 2:c % 2 + 1], vec[:, D:2 * D], ALU.mult,
                                         ALU.add).then_inc(v_n, 1)

            dve.wait_ge(p_set, 3)
            stack_k(0, 0)
            dve.wait_ge(p_r1, 1)
            normalise(0, 0)
            normalise(0, 1)
            stack_q(0, 0)
            negmax(0, 0)
            negmax(0, 1)
            dve.wait_ge(a_tg, 1)

            def pair(i):
                for w in range(8):
                    c, s = divmod(w, SETS)
                    if s == 0 and has(i, c + 1):
                        stack_k(i, c + 1)
                    if s == 1 and has(i, c + 1):
                        stack_q(i, c + 1)
                    if has(i, (w + 2) // SETS):
                        negmax(i, w + 2)
                    if s == 0 and has(i, c - 2):
                        residual(i, c - 2)
                    if s == 0 and has(i, c + 2):
                        normalise(i, c + 2)
                    if s == 1 and has(i, c - 2):
                        normed(i, c - 2)
                    if s == 1 and has(i, c - 1):
                        weigh(i, c - 1)
            over_pairs(dve, pair)
            last = B - 2
            residual(last, 0)
            weigh(last, 1)
            normed(last, 0)
            residual(last, 1)
            normed(last, 1)

            steps = [0]

            def link(ins):
                steps[0] += 1
                ins.then_inc(v_rt, 1)
                dve.wait_ge(v_rt, steps[0])

            def wide(a):
                return a.unsqueeze(2).to_broadcast((T, B, E))

            lgp = LG[:, 0:B * E].rearrange("p (b e) -> p b e", b=B)
            dve.wait_ge(pe_lg, 1)
            link(dve.tensor_reduce(col["mx"][:, :], lgp, AX, ALU.max))
            link(dve.tensor_tensor(lg[:, :, :], lgp, wide(col["mx"][:, :]), ALU.subtract))
            dve.wait_ge(a_ex, 1)
            link(dve.tensor_reduce(col["sum"][:, :], ex[:, :, :], AX, ALU.add))
            link(dve.reciprocal(col["rs"][:, :], col["sum"][:, :]))
            link(dve.tensor_tensor(pr[:, :, :], ex[:, :, :], wide(col["rs"][:, :]), ALU.mult))
            for n, src in ((0, pr), (1, pr2)):
                p, wn = col[f"p{n + 1}"], col[f"w{n + 1}"]
                if n:
                    link(dve.scalar_tensor_tensor(pr2[:, :, :], M[:, 0], -2.0, pr[:, :, :], ALU.mult, ALU.add))
                link(dve.tensor_reduce(p[:, :], src[:, :, :], AX, ALU.max))
                link(dve.tensor_tensor(eq[:, n], src[:, :, :], wide(p[:, :]), ALU.is_equal))
                link(dve.tensor_tensor(ew[:, n], eq[:, n], cst[:, C_EW:C_EW + E].unsqueeze(1).to_broadcast((T, B, E)), ALU.mult))
                link(dve.tensor_reduce(wn[:, :], ew[:, n], AX, ALU.max))
                link(dve.tensor_tensor(M[:, n], ew[:, n], wide(wn[:, :]), ALU.is_equal))
            dve.wait_ge(p_set, 3)
            link(dve.tensor_tensor(Mb[:, 0:B, :], M[:, 0], M[:, 1], ALU.add))
            assert steps[0] == V_MB
            link(dve.tensor_tensor(col["dp"][:, :], col["p2"][:, :], col["p1"][:, :], ALU.subtract))
            assert steps[0] == V_DP
            dve.wait_ge(pe_rank, 1)
            rank = RK[:, 0:(B + 1) * E].rearrange("p (b e) -> p b e", e=E)
            link(dve.tensor_tensor(over[:, :, :], rank[:, B, :].unsqueeze(2).to_broadcast((T, E, E)),
                                   cst[:, C_J:C_J + E].unsqueeze(1).to_broadcast((T, E, E)), ALU.is_gt))
            link(dve.tensor_reduce(nt[:, :], over[:, :, :], AX, ALU.add))
            link(dve.tensor_tensor_scan(inc[:, :], cst[:, C_ON:C_ON + 1].to_broadcast((T, E)), nt[:, :], 0.0, ALU.mult, ALU.add))
            link(dve.tensor_tensor(ts[:, :], inc[:, :], nt[:, :], ALU.subtract))
            link(dve.tensor_scalar(base[:, :], ts[:, :], float(T), None, ALU.mult))
            link(dve.tensor_tensor(dest[:, :, :], rank[:, 0:B, :], base[:, :].unsqueeze(1).to_broadcast((T, B, E)), ALU.add))
            for n in range(2):
                link(dve.tensor_tensor(md[:, n], M[:, n], dest[:, :, :], ALU.mult))
            link(dve.tensor_reduce(slot[:, :, :], md[:, :, :, :], AX, ALU.add))
            link(dve.tensor_copy(sloti[:, :, :], slot[:, :, :]))
            link(dve.tensor_scalar(inti[:, 1], sloti[:, :, :], T.bit_length() - 1, None, ALU.arith_shift_right))
            link(dve.tensor_tensor(tiles_of[:, :, :], cst[:, C_TL:C_TL + TT].unsqueeze(1).to_broadcast((T, 2 * B, TT)),
                                   inti[:, 1].rearrange("p k b -> p (k b)").unsqueeze(2).to_broadcast((T, 2 * B, TT)), ALU.is_equal))
            assert steps[0] == V_TI
            link(dve.tensor_scalar(inti[:, 0], sloti[:, :, :], T - 1, None, ALU.bitwise_and))
            link(dve.tensor_copy(intb[:, :], inti[:, 0].rearrange("p k b -> p (k b)")))
            link(dve.tensor_tensor(Aoh[:, :, :], slotb[:, :].unsqueeze(1).to_broadcast((T, 2 * B, T)),
                                   intb[:, :].unsqueeze(2).to_broadcast((T, 2 * B, T)), ALU.is_equal))
            assert steps[0] == V_AOH
            link(dve.tensor_tensor(cmpe[:, :, 0:E - 1], cst[0:1, C_TL:C_TL + TT].unsqueeze(2).to_broadcast((1, TT, E - 1)),
                                   ts[0:1, 1:E].unsqueeze(1).to_broadcast((1, TT, E - 1)), ALU.is_ge))
            link(dve.tensor_reduce(eidf[:, :], cmpe[:, :, 0:E - 1], AX, ALU.add))
            link(dve.tensor_scalar(goff[:, :], eidf[:, :], float(GU), None, ALU.mult))
            dve.wait_ge(a_e2, 1)
            link(dve.tensor_scalar(col["o2"][:, :], col["e2"][:, :], 1.0, None, ALU.add))
            link(dve.reciprocal(col["g1"][:, :], col["o2"][:, :]))
            link(dve.tensor_scalar(col["g1"][:, :], col["g1"][:, :], tg[:, 1:2], None, ALU.mult))
            link(dve.tensor_tensor(col["g2"][:, :], col["e2"][:, :], col["g1"][:, :], ALU.mult))
            dve.wait_ge(pe_tab, 1)
            tab = TAB[:, 0:2 * TT].rearrange("p (n i) -> p n i", n=2)
            link(dve.tensor_reduce(id1[:, :], tab.rearrange("p n i -> p i n"), AX, ALU.add))
            link(dve.tensor_scalar(gi[:, :], id1[:, :], -1.0, 0.0, ALU.add, ALU.max))
            link(dve.tensor_copy(gidx[:, :], gi[:, :]))
            link(dve.tensor_scalar(gtok[:, :], gidx[:, :], 1, None, ALU.arith_shift_right))
            link(dve.tensor_scalar(none[:, :], id1[:, :], 0.0, SKIP, ALU.is_equal, ALU.mult))
            link(dve.tensor_tensor(si[:, :], gi[:, :], none[:, :], ALU.add))
            dve.tensor_copy(sidx[:, :], si[:, :]).then_inc(v_ready, 1)

            def tok_lo(n, m):
                done(dve, a_gh, n, m)
                done(dve, pe_gu, n, m - 2)
                dve.tensor_tensor(gTl[:, m % 2, :], bank[4][:, 0:T], gTh[:, m % 2, :].bitcast(f32),
                                  ALU.subtract).then_inc(v_gl[m % 4], 1)

            def in_indices(n, m):
                done(dve, gat, n, m - 4, 16)
                dve.tensor_copy(gring[:, m % 4:m % 4 + 1], gtok[:, bass.ds(4 * n + m, 1)]).then_inc(v_gi[m % 4], 1)

            def out_indices(n, m):
                done(dve, sca, n, m - 2, 16)
                dve.tensor_copy(sring[:, m % 2:m % 2 + 1], sidx[:, bass.ds(4 * n + m, 1)]).then_inc(v_si[m % 4], 1)

            for m in range(4):
                in_indices(0, m)
            tok_lo(0, 0)

            def step(n, m):
                if tile_in(n, m + 1):
                    tok_lo(n, m + 1)
                if tile_in(n, m + 4):
                    in_indices(n, m + 4)
                if tile_in(n, m - 2):
                    out_indices(n, m - 2)
                if tile_in(n, m):
                    done(dve, a_s, n, m)
                    dve.tensor_tensor(gH[:, m % 2, :], gS[:, m % 2, :], bank[2 + m % 2][:, 0:F], ALU.mult).then_inc(v_h[m % 4], 1)
            over_tiles(dve, step)

            dve.wait_ge(v_rt, steps[0])
            dve.wait_ge(p_x3, 2)
            for h in range(B // 2):
                dve.wait_ge(ld_y[h], 16)
                bs = (2 * h, 2 * h + 1)
                for b in bs:
                    dve.scalar_tensor_tensor(YG[:, b, 0, :], YG[:, b, 0, :], col["g1"][:, b:b + 1], X2[:, b * D:(b + 1) * D],
                                             ALU.mult, ALU.add).then_inc(v_f1, 1)
                for b in bs:
                    dve.wait_ge(v_f1, b + 1)
                    dve.scalar_tensor_tensor(out_sb[:, b, :], YG[:, b, 1, :], col["g2"][:, b:b + 1], YG[:, b, 0, :],
                                             ALU.mult, ALU.add).then_inc(v_out, 1)

        @block.tensor
        def _(pe):
            ident = cst[:, C_ID:C_ID + T]

            def x_T(i, c):
                seq_done(pe, v_xn, i, c)
                seq_done(pe, v_q, i, c - 1)
                pe.transpose(Qb[:, 0:T], xn[:, c % 2, :], ident).then_inc(pe_xT, 1)

            def queries(i, c):
                seq_done(pe, a_xT, i, c)
                seq_done(pe, v_kc, i, c)
                for s in range(SETS):
                    last = pe.matmul(Qb[:, s * T:(s + 1) * T], wstk[:, 0, s, :], xT[:, :], start=True, stop=True)
                last.then_inc(pe_q, 1)

            def keys(i, c):
                load_done(pe, ld_c, i, c)
                seq_done(pe, a_xT, i, c)
                for s in range(SETS):
                    last = pe.matmul(Qb[:, s * T:(s + 1) * T], wstk[:, 1, s, :], cT[:, c % 2, :], start=True, stop=True)
                last.then_inc(pe_k, 1)

            def val_proj(i, c):
                seq_done(pe, v_x2, i, c - 3)
                pe.matmul(Mi[:, 0:D], cT[:, c % 2, :], wsm[:, WV:WV + D], start=True, stop=True).then_inc(pe_v, 1)

            def scores(i, w):
                c, s = divmod(w, SETS)
                if s == 0:
                    seq_done(pe, v_q, i, c)
                    seq_done(pe, v_k, i, c)
                    load_done(pe, st_k, i, c, 2)
                pe.matmul(Sb[w % 4][:, :], identb[:, :], maskb[:, :, :].rearrange("p s t -> p (s t)"), start=True, stop=False)
                pe.matmul(Sb[w % 4][:, :], qS[:, c % 2, s, :], kS[:, c % 2, s].rearrange("p j t -> p (j t)"), start=False,
                          stop=True).then_inc(pe_S[w % 4], 1)

            def weights_T(i, w):
                unit_done(pe, a_exp, i, w)
                unit_done(pe, a_PT, i, w - 1)
                if w % SETS in WARM_SETS:
                    pe.matmul(Tb[:, :], identb[:, :], maskb[:, :, :].rearrange("p s t -> p (s t)"), start=True, stop=True)
                for j in range(ROWS):
                    last = pe.transpose(Tb[:, j * T:(j + 1) * T], P[:, w % 2, j, :], ident)
                last.then_inc(pe_T[w % 4], 1)

            def values(i, w):
                c, s = divmod(w, SETS)
                if s == 0:
                    seq_done(pe, a_v, i, c)
                    seq_done(pe, v_att, i, c - 1)
                for j in range(ROWS):
                    h = ROWS * s + j
                    last = pe.matmul(Ob[:, h * (HD + 1):(h + 1) * (HD + 1)], PT[:, w % 2, j, :], V[:, c % 2, h, :],
                                     start=(s == 0 and j == 0), stop=(s == SETS - 1 and j == ROWS - 1))
                last.then_inc(pe_PV[w % 4], 1)

            def att_T(i, c):
                seq_done(pe, v_att, i, c)
                pe.transpose(Mi[:, 0:T], att[:, :], ident).then_inc(pe_aT, 1)

            def out_proj(i, c):
                seq_done(pe, a_aT, i, c)
                pe.matmul(Mi[:, 0:D], aT[:, :], wsm[:, WO:WO + D], start=True, stop=True).then_inc(pe_wo, 1)

            def n_T(i, c):
                seq_done(pe, v_n, i, c)
                pe.transpose(Qb[:, 0:T], nr[:, c % 2, :], ident).then_inc(pe_nT, 1)

            pe.wait_ge(v_setup, 2 + 2 * COPIES)
            load_done(pe, ld_c, 0, 0)
            for s in range(SETS):
                last = pe.matmul(Qb[:, s * T:(s + 1) * T], wstk[:, 1, s, :], cT[:, 0, :], start=True, stop=True)
            last.then_inc(pe_k, 1)
            val_proj(0, 0)
            seq_done(pe, v_kc, 0, 0)
            x_T(0, 0)
            queries(0, 0)
            pe.wait_ge(p_set, 4)
            pe.wait_ge(v_setup, 2 + 2 * COPIES + 5)
            scores(0, 0)
            scores(0, 1)
            x_T(0, 1)
            keys(0, 1)

            def pair(i):
                for w in range(8):
                    c, s = divmod(w, SETS)
                    if not isinstance(i, int) or 4 * i + w >= 1:
                        weights_T(i, w - 1)
                    if has(i, (w + 2) // SETS):
                        scores(i, w + 2)
                    if not isinstance(i, int) or 4 * i + w >= 2:
                        values(i, w - 2)
                    if s == 0 and has(i, c + 1):
                        queries(i, c + 1)
                    if s == 1 and has(i, c + 2):
                        x_T(i, c + 2)
                    if s == 1 and has(i, c + 1):
                        val_proj(i, c + 1)
                    if s == 2 and has(i, c - 2):
                        if has(i, c + 2):
                            seq_done(pe, a_xT, i, c + 2)
                        n_T(i, c - 2)
                    if s == 2 and has(i, c - 1):
                        if has(i, c + 1):
                            seq_done(pe, a_v, i, c + 1)
                        att_T(i, c - 1)
                    if s == 3 and has(i, c - 1):
                        out_proj(i, c - 1)
                    if s == 3 and has(i, c + 2):
                        seq_done(pe, a_nT, i, c - 2)
                        keys(i, c + 2)
            over_pairs(pe, pair)
            last = B - 2

            def logits(b):
                pe.wait_ge(a_nT, b + 1)
                mm = pe.matmul(LG[:, b * E:(b + 1) * E], NT[:, b * T:(b + 1) * T], wsm[:, WR:WR + E], start=(b == 0),
                               stop=(b == B - 1))
                if b == B - 1:
                    mm.then_inc(pe_lg, 1)

            def shared_gate_up(h):
                for o, bk in ((WSG, SG[h]), (WSU, SU[h])):
                    pe.matmul(bk[:, :], wsm[:, o:o + SF], NT[:, h * HALF:(h + 1) * HALF], start=True, stop=True).then_inc(pe_sgu, 1)

            weights_T(last, 7)
            values(last, 6)
            logits(0)
            logits(1)
            unit_done(pe, a_PT, last, 7)
            values(last, 7)
            for b in range(2, B - 2):
                logits(b)
            seq_done(pe, v_x2, last, 0)
            att_T(last, 1)
            n_T(last, 0)
            out_proj(last, 1)
            shared_gate_up(0)
            seq_done(pe, a_nT, last, 0)
            n_T(last, 1)

            logits(B - 2)
            logits(B - 1)
            shared_gate_up(1)

            pe.wait_ge(v_rt, V_MB)
            mb = Mb[:, :, :].rearrange("p b e -> p (b e)")
            pe.matmul(RK[:, 0:(B + 1) * E], ltb[:, :], mb, start=True, stop=False)
            for s in range(1, B + 1):
                last = pe.matmul(RK[:, s * E:(B + 1) * E], onesb[:, :], mb[:, 0:(B + 1 - s) * E], start=False, stop=(s == B))
            last.then_inc(pe_rank, 1)
            for h in range(2):
                pe.wait_ge(p_sh, h + 1)
                for b in range(B // 2):
                    t = h * HALF + b * T
                    last = pe.matmul(SY[h][:, b * D:(b + 1) * D], sH[:, t:t + T], wsm[:, WSD:WSD + D], start=True, stop=True)
                last.then_inc(pe_sy, 1)
            pe.wait_ge(v_rt, V_AOH)
            pe.wait_ge(p_bv, 2)
            for n in range(2 * B):
                last = pe.matmul(TAB[:, 0:2 * TT], Aoh[:, n, :], Bv[:, n].rearrange("p n i -> p (n i)"), start=(n == 0),
                                 stop=(n == 2 * B - 1))
            last.then_inc(pe_tab, 1)

            def tok_T(n, m):
                done(pe, gat, n, m, 16)
                pe.transpose(bank[4][:, 0:T], XG[:, m % 4, :], ident).then_inc(pe_gT[m % 4], 1)

            offsets = {}

            def place(n, m):
                return 4 * n + m if isinstance(n, int) else ("loop", m)

            def load_offset(n, m):
                offsets[place(n, m)] = pe.value_load(goff[0:1, bass.ds(4 * n + m, 1)], min_val=0, max_val=(E - 1) * GU)

            pe.wait_ge(a_sy, 2)
            pe.wait_ge(ld_d, 16)
            pe.wait_ge(p_wl, E)
            tok_T(0, 0)

            def step(n, m):
                if tile_in(n, m):
                    if place(n, m) not in offsets:
                        load_offset(n, m)
                    e = offsets[place(n, m)]
                    done(pe, v_gl, n, m)
                    if tile_in(n, m + 1):
                        tok_T(n, m + 1)
                    gh, gl = gTh[:, m % 2, :], gTl[:, m % 2, :]
                    for o, bk in ((0, bank[m % 2]), (F, bank[2 + m % 2])):
                        w = bass.ds(e + o, F)
                        pe.matmul(bk[:, 0:F], gh, WH[:, w], start=True, stop=False)
                        pe.matmul(bk[:, 0:F], gl, WH[:, w], start=False, stop=False)
                        last = pe.matmul(bk[:, 0:F], gh, WL[:, w], start=False, stop=True)
                    last.then_inc(pe_gu[m % 4], 1)
                if tile_in(n, m - 2):
                    if place(n, m - 2) not in offsets:
                        load_offset(n, m - 2)
                    e = offsets.pop(place(n, m - 2))
                    done(pe, a_hT, n, m - 2)
                    done(pe, a_y, n, m - 3)
                    for f in range(FC):
                        last = pe.matmul(bank[7][:, 0:D], hT[:, m % 2, f * T:(f + 1) * T], WD[:, bass.ds(e + f * D, D)],
                                         start=(f == 0), stop=(f == FC - 1))
                    last.then_inc(pe_y[(m - 2) % 4], 1)
                if tile_in(n, m + 1) and m % 4 != 3:
                    load_offset(n, m + 1)
                if tile_in(n, m - 1):
                    done(pe, v_h, n, m - 1)
                    for f in range(FC):
                        last = pe.transpose(bank[5 + (m - 1) % 2][:, f * T:(f + 1) * T], gH[:, (m - 1) % 2, f * T:(f + 1) * T], ident)
                    last.then_inc(pe_hT[(m - 1) % 4], 1)
            over_tiles(pe, step)


V_MB = 5 + 5 + 6 + 1
V_DP = V_MB + 1
V_TI = V_DP + 6 + 3 + 3
V_AOH = V_TI + 3


def kernel(**inputs):
    import numpy as _np
    import concourse.bacc as _bacc
    from concourse import mybir as _mybir
    from concourse.bass_utils import run_bass_kernel_spmd as _run

    a = {k: _np.asarray(v) for k, v in inputs.items()}
    p = _np.arange(T)
    const = _np.zeros((T, CONST), _np.float32)
    const[:, C_ID:C_ID + T] = p[:, None] == p[None, :]
    const[:, C_LT:C_LT + T] = p[:, None] < p[None, :]
    const[:, C_CM:C_CM + T] = _np.where(p[:, None] >= p[None, :], 0.0, -1e30)
    const[:, C_SL:C_SL + T] = p
    const[:, C_TL:C_TL + TT] = _np.arange(TT)
    const[:, C_LQ] = (p % 32) // HD == 1
    const[:, C_LK] = (p % 32) // HD == 2
    const[:, C_EW:C_EW + E] = E - _np.arange(E)
    const[:, C_J:C_J + E] = T * _np.arange(E)
    kk = _np.repeat(_np.arange(2), B)
    const[:, C_PK:C_PK + 2 * B] = 2 * p[:, None] + kk[None, :] + 1
    const[:, C_TK:C_TK + 2 * B] = 2 * T * _np.tile(_np.arange(B), 2)
    const[:, C_ON:C_ON + 2] = 1.0
    wsmall = _np.concatenate([a[n].T for n in ("L0_xattn_Wq", "L0_xattn_Wk", "L0_xattn_Wv", "L0_xattn_Wo",
                                               "L0_ffn_shared_gate_up_w", "L0_ffn_shared_down_w", "L0_ffn_router_w")], axis=1)
    gu = a["L0_ffn_gate_up_w"].transpose(0, 2, 1)
    dn = a["L0_ffn_down_w"].transpose(0, 2, 1).reshape(E, FC, T, D).transpose(0, 2, 1, 3).transpose(1, 0, 2, 3).reshape(T, E * FC * D)
    arrays = {
        "x": a["x"].reshape(B * T, D),
        "ctxT": a["ctx_1024"].reshape(B * T, D).T,
        "vec": _np.concatenate([a["L0_ffn_ln_gamma"], a["L0_ffn_ln_beta"], a["g_xattn"], a["g_ffn"]])[None, :],
        "wsmall": wsmall,
        "wgu": gu.reshape(E * D, GU),
        "wdn": dn,
        "const": const,
    }
    nc = _bacc.Bacc("TRN2", target_bir_lowering=False, num_devices=1)
    ins, args = {}, []
    for name, v in arrays.items():
        ins["in_" + name] = _np.ascontiguousarray(v)
        args.append(nc.dram_tensor("in_" + name, v.shape, _mybir.dt.from_np(v.dtype), kind="ExternalInput").ap())
    args.append(nc.dram_tensor("out", (B * T, D), _mybir.dt.float32, kind="ExternalOutput").ap())
    gated_layer(nc, *args)
    r = _run(nc, [ins], core_ids=[0])
    return r.results[0]["out"].reshape(B, T, D)
```
